# Optimizing a Trainium2 kernel written in Bass

```python
import numpy as np
import jax
import jax.numpy as jnp

def _softmax(x, axis=-1):
    return jax.nn.softmax(x, axis=axis)

def _gelu(x):
    return jax.nn.gelu(x, approximate=True)

def _silu(x):
    return jax.nn.silu(x)

def _sigmoid(x):
    return jax.nn.sigmoid(x)

def _layernorm(x, axis=-1, eps=1e-05):
    m = jnp.mean(x, axis=axis, keepdims=True)
    v = jnp.var(x, axis=axis, keepdims=True)
    return (x - m) / jnp.sqrt(v + eps)

def _scatter_add(tgt, idx, src, axis=0):
    return tgt.at[idx].add(src)

def _segment_sum(src, seg, n):
    return jax.ops.segment_sum(src, seg, n)
kernel_name = 'mk_macaron_d1_jaxref_r8_60bd49'

def setup_inputs(seed: int=0):
    np.random.seed(seed)
    _w = jnp.asarray

    def _L0_attn_setup():
        import jax, jax.numpy as jnp
        import numpy as np
        D = 128
        key = jax.random.key(seed)
        k0, k1, k2, k3 = jax.random.split(key, 4)
        x = jax.random.normal(k0, (4, 256, D), dtype=jnp.float32)
        Wk = jax.random.normal(k1, (D, D), dtype=jnp.float32) * 0.02
        Wq = jax.random.normal(k2, (D, D), dtype=jnp.float32) * 0.02
        Wv = jax.random.normal(k3, (D, D), dtype=jnp.float32) * 0.02
        return {'x': x, 'Wk': Wk, 'Wq': Wq, 'Wv': Wv}
    _L0_attn_in = _L0_attn_setup()

    def _L0_ffn_setup():
        import jax, jax.numpy as jnp
        import numpy as np
        DIM = 128
        DEPTH = 2
        HEADS = 8
        DIM_HEAD = 64
        WINDOW = 64
        INNER = HEADS * DIM_HEAD
        HID = int(DIM * 4 * 2 / 3)
        B, N = (2, 1024)
        QK_SCALE = 8.0

        def shift_token(t):
            t1, t2 = jnp.split(t, 2, axis=-1)
            t2 = jnp.pad(t2, ((0, 0), (1, 0), (0, 0)))[:, :-1]
            return jnp.concatenate([t1, t2], axis=-1)

        def l2norm(t):
            return t / jnp.clip(jnp.linalg.norm(t, axis=-1, keepdims=True), 1e-12)

        def rotate_half(x):
            x1, x2 = jnp.split(x, 2, axis=-1)
            return jnp.concatenate([-x2, x1], axis=-1)

        def rotary_xpos(q, k):
            n = q.shape[-2]
            half_idx = jnp.arange(0, DIM_HEAD, 2, dtype=jnp.float32)
            inv_freq = 1.0 / 10000.0 ** (half_idx / DIM_HEAD)
            t = jnp.arange(n, dtype=jnp.float32)
            freqs = t[:, None] * inv_freq[None, :]
            freqs = jnp.concatenate([freqs, freqs], axis=-1)
            base = (half_idx + 0.4 * DIM_HEAD) / (1.4 * DIM_HEAD)
            power = (t - n // 2) / float(WINDOW // 2)
            scale = base[None, :] ** power[:, None]
            scale = jnp.concatenate([scale, scale], axis=-1)
            cos, sin = (jnp.cos(freqs), jnp.sin(freqs))
            q = q * cos * scale + rotate_half(q) * sin * scale
            k = k * cos / scale + rotate_half(k) * sin / scale
            return (q, k)

        def local_attention(q, k, v):
            b, h, n, d = q.shape
            w = n // WINDOW
            bq = q.reshape(b, h, w, WINDOW, d) * QK_SCALE
            bk = k.reshape(b, h, w, WINDOW, d)
            bv = v.reshape(b, h, w, WINDOW, d)

            def look_around(t):
                p = jnp.pad(t, ((0, 0), (0, 0), (1, 0), (0, 0), (0, 0)))
                return jnp.concatenate([p[:, :, :w], p[:, :, 1:]], axis=3)
            bk, bv = (look_around(bk), look_around(bv))
            bt = jnp.arange(n).reshape(w, WINDOW)
            btp = jnp.pad(bt, ((1, 0), (0, 0)), constant_values=-1)
            btk = jnp.concatenate([btp[:w], btp[1:]], axis=1)
            sim = jnp.einsum('bhwid,bhwjd->bhwij', bq, bk)
            i = bt[:, :, None]
            j = btk[:, None, :]
            mask = (i < j) | (i > j + WINDOW) | (j == -1)
            sim = jnp.where(mask, -jnp.finfo(sim.dtype).max, sim)
            attn = jax.nn.softmax(sim, axis=-1)
            out = jnp.einsum('bhwij,bhwjd->bhwid', attn, bv)
            return out.reshape(b, h, n, d)

        def _layer(x, wqkv, qs, ksc, wo, lg, lb, w1, b1, w2, b2):
            b, n, _ = x.shape
            h = shift_token(x)
            qkv = h @ wqkv
            q, k, v = jnp.split(qkv, 3, axis=-1)
            to_heads = lambda t: t.reshape(b, n, HEADS, DIM_HEAD).transpose(0, 2, 1, 3)
            q, k, v = (to_heads(q), to_heads(k), to_heads(v))
            q = l2norm(q) * qs
            k = l2norm(k) * ksc
            q, k = rotary_xpos(q, k)
            o = local_attention(q, k, v)
            o = o.transpose(0, 2, 1, 3).reshape(b, n, INNER)
            x = x + o @ wo
            h = shift_token(x)
            mu = h.mean(-1, keepdims=True)
            var = h.var(-1, keepdims=True)
            h = (h - mu) / jnp.sqrt(var + 1e-05) * lg + lb
            h = h @ w1 + b1
            a, g = jnp.split(h, 2, axis=-1)
            h = a * jax.nn.gelu(g, approximate=False)
            x = x + h @ w2 + b2
            return x
        key = jax.random.key(seed)
        ks = jax.random.split(key, 6)
        return {'x': jax.random.normal(ks[0], (B, N, DIM), jnp.float32), 'wqkv': jax.random.normal(ks[1], (DEPTH, DIM, 3 * INNER), jnp.float32) * 0.02, 'q_scale': jnp.ones((DEPTH, DIM_HEAD), jnp.float32), 'k_scale': jnp.ones((DEPTH, DIM_HEAD), jnp.float32), 'wo': jax.random.normal(ks[2], (DEPTH, INNER, DIM), jnp.float32) * 0.02, 'ln_g': jnp.ones((DEPTH, DIM), jnp.float32), 'ln_b': jnp.zeros((DEPTH, DIM), jnp.float32), 'w1': jax.random.normal(ks[3], (DEPTH, DIM, 2 * HID), jnp.float32) * 0.02, 'b1': jnp.zeros((DEPTH, 2 * HID), jnp.float32), 'w2': jax.random.normal(ks[4], (DEPTH, HID, DIM), jnp.float32) * 0.02, 'b2': jnp.zeros((DEPTH, DIM), jnp.float32)}
    _L0_ffn_in = _L0_ffn_setup()
    _d = {'L0_attn_x': _L0_attn_in['x'], 'L0_attn_Wk': _L0_attn_in['Wk'], 'L0_attn_Wq': _L0_attn_in['Wq'], 'L0_attn_Wv': _L0_attn_in['Wv'], 'L0_ffn_wqkv': _L0_ffn_in['wqkv'], 'L0_ffn_q_scale': _L0_ffn_in['q_scale'], 'L0_ffn_k_scale': _L0_ffn_in['k_scale'], 'L0_ffn_wo': _L0_ffn_in['wo'], 'L0_ffn_ln_g': _L0_ffn_in['ln_g'], 'L0_ffn_ln_b': _L0_ffn_in['ln_b'], 'L0_ffn_w1': _L0_ffn_in['w1'], 'L0_ffn_b1': _L0_ffn_in['b1'], 'L0_ffn_w2': _L0_ffn_in['w2'], 'L0_ffn_b2': _L0_ffn_in['b2']}
    _x0 = _d['L0_attn_x']
    _d['L0_attn_x'] = jax.random.normal(jax.random.fold_in(jax.random.key(seed), 1), (8, 1024, 128), dtype=_x0.dtype)
    del _x0
    return _d

def reference(L0_attn_x, L0_attn_Wk, L0_attn_Wq, L0_attn_Wv, L0_ffn_wqkv, L0_ffn_q_scale, L0_ffn_k_scale, L0_ffn_wo, L0_ffn_ln_g, L0_ffn_ln_b, L0_ffn_w1, L0_ffn_b1, L0_ffn_w2, L0_ffn_b2):

    def _L0_attn_ref(x, Wk, Wq, Wv):
        import jax, jax.numpy as jnp
        import numpy as np
        D = 128
        K = x @ Wk
        Q = x @ Wq
        V = x @ Wv
        N = Q.shape[-2]
        d = K.shape[-1]
        scores = jnp.einsum('bnd,bmd->bnm', Q, K) / jnp.sqrt(jnp.float32(d))
        causal = jnp.tril(jnp.ones((N, N), dtype=bool))
        scores = jnp.where(causal[None, :, :], scores, -jnp.inf)
        attn = jax.nn.softmax(scores, axis=-1)
        return attn @ V

    def _L0_ffn_ref(x, wqkv, q_scale, k_scale, wo, ln_g, ln_b, w1, b1, w2, b2):
        import jax, jax.numpy as jnp
        import numpy as np
        DIM = 128
        DEPTH = 2
        HEADS = 8
        DIM_HEAD = 64
        WINDOW = 64
        INNER = HEADS * DIM_HEAD
        HID = int(DIM * 4 * 2 / 3)
        B, N = (2, 1024)
        QK_SCALE = 8.0

        def shift_token(t):
            t1, t2 = jnp.split(t, 2, axis=-1)
            t2 = jnp.pad(t2, ((0, 0), (1, 0), (0, 0)))[:, :-1]
            return jnp.concatenate([t1, t2], axis=-1)

        def l2norm(t):
            return t / jnp.clip(jnp.linalg.norm(t, axis=-1, keepdims=True), 1e-12)

        def rotate_half(x):
            x1, x2 = jnp.split(x, 2, axis=-1)
            return jnp.concatenate([-x2, x1], axis=-1)

        def rotary_xpos(q, k):
            n = q.shape[-2]
            half_idx = jnp.arange(0, DIM_HEAD, 2, dtype=jnp.float32)
            inv_freq = 1.0 / 10000.0 ** (half_idx / DIM_HEAD)
            t = jnp.arange(n, dtype=jnp.float32)
            freqs = t[:, None] * inv_freq[None, :]
            freqs = jnp.concatenate([freqs, freqs], axis=-1)
            base = (half_idx + 0.4 * DIM_HEAD) / (1.4 * DIM_HEAD)
            power = (t - n // 2) / float(WINDOW // 2)
            scale = base[None, :] ** power[:, None]
            scale = jnp.concatenate([scale, scale], axis=-1)
            cos, sin = (jnp.cos(freqs), jnp.sin(freqs))
            q = q * cos * scale + rotate_half(q) * sin * scale
            k = k * cos / scale + rotate_half(k) * sin / scale
            return (q, k)

        def local_attention(q, k, v):
            b, h, n, d = q.shape
            w = n // WINDOW
            bq = q.reshape(b, h, w, WINDOW, d) * QK_SCALE
            bk = k.reshape(b, h, w, WINDOW, d)
            bv = v.reshape(b, h, w, WINDOW, d)

            def look_around(t):
                p = jnp.pad(t, ((0, 0), (0, 0), (1, 0), (0, 0), (0, 0)))
                return jnp.concatenate([p[:, :, :w], p[:, :, 1:]], axis=3)
            bk, bv = (look_around(bk), look_around(bv))
            bt = jnp.arange(n).reshape(w, WINDOW)
            btp = jnp.pad(bt, ((1, 0), (0, 0)), constant_values=-1)
            btk = jnp.concatenate([btp[:w], btp[1:]], axis=1)
            sim = jnp.einsum('bhwid,bhwjd->bhwij', bq, bk)
            i = bt[:, :, None]
            j = btk[:, None, :]
            mask = (i < j) | (i > j + WINDOW) | (j == -1)
            sim = jnp.where(mask, -jnp.finfo(sim.dtype).max, sim)
            attn = jax.nn.softmax(sim, axis=-1)
            out = jnp.einsum('bhwij,bhwjd->bhwid', attn, bv)
            return out.reshape(b, h, n, d)

        def _layer(x, wqkv, qs, ksc, wo, lg, lb, w1, b1, w2, b2):
            b, n, _ = x.shape
            h = shift_token(x)
            qkv = h @ wqkv
            q, k, v = jnp.split(qkv, 3, axis=-1)
            to_heads = lambda t: t.reshape(b, n, HEADS, DIM_HEAD).transpose(0, 2, 1, 3)
            q, k, v = (to_heads(q), to_heads(k), to_heads(v))
            q = l2norm(q) * qs
            k = l2norm(k) * ksc
            q, k = rotary_xpos(q, k)
            o = local_attention(q, k, v)
            o = o.transpose(0, 2, 1, 3).reshape(b, n, INNER)
            x = x + o @ wo
            h = shift_token(x)
            mu = h.mean(-1, keepdims=True)
            var = h.var(-1, keepdims=True)
            h = (h - mu) / jnp.sqrt(var + 1e-05) * lg + lb
            h = h @ w1 + b1
            a, g = jnp.split(h, 2, axis=-1)
            h = a * jax.nn.gelu(g, approximate=False)
            x = x + h @ w2 + b2
            return x
        for l in range(DEPTH):
            x = _layer(x, wqkv[l], q_scale[l], k_scale[l], wo[l], ln_g[l], ln_b[l], w1[l], b1[l], w2[l], b2[l])
        return x
    x = L0_attn_x
    x = x + 0.5 * _L0_ffn_ref(_layernorm(x, axis=-1), L0_ffn_wqkv, L0_ffn_q_scale, L0_ffn_k_scale, L0_ffn_wo, L0_ffn_ln_g, L0_ffn_ln_b, L0_ffn_w1, L0_ffn_b1, L0_ffn_w2, L0_ffn_b2)
    x = x + _L0_attn_ref(_layernorm(x, axis=-1), L0_attn_Wk, L0_attn_Wq, L0_attn_Wv)
    x = x + 0.5 * _L0_ffn_ref(_layernorm(x, axis=-1), L0_ffn_wqkv, L0_ffn_q_scale, L0_ffn_k_scale, L0_ffn_wo, L0_ffn_ln_g, L0_ffn_ln_b, L0_ffn_w1, L0_ffn_b1, L0_ffn_w2, L0_ffn_b2)
    return x

_drawn_inputs = setup_inputs


def setup_inputs(seed=0):
    import zlib

    import numpy as np

    out = dict(_drawn_inputs(seed))
    spreads = {'L0_ffn_q_scale': (1.0, 0.6),
     'L0_ffn_k_scale': (1.0, 0.6),
     'L0_ffn_ln_g': (1.0, 0.6),
     'L0_ffn_ln_b': (0.0, 0.8),
     'L0_ffn_b1': (0.0, 0.8),
     'L0_ffn_b2': (0.0, 0.1)}
    factors = {'L0_attn_Wk': 8.0,
     'L0_attn_Wq': 8.0,
     'L0_attn_Wv': 3.794,
     'L0_ffn_wqkv': 3.327,
     'L0_ffn_wo': 3.308,
     'L0_ffn_w1': 5.301,
     'L0_ffn_w2': 5.221}
    for name, (base, spread) in spreads.items():
        noise = np.random.default_rng([zlib.crc32(name.encode()), seed]).standard_normal(out[name].shape)
        drawn = base * np.exp(spread * noise) if base else spread * noise
        out[name] = jnp.asarray(drawn.astype(out[name].dtype))
    for name, factor in factors.items():
        out[name] = (out[name] * factor).astype(out[name].dtype)
    return out
```

```python
import numpy as np
import concourse.bass as bass
from concourse import mybir

F32 = mybir.dt.float32
BF16 = mybir.dt.bfloat16
ALU = mybir.AluOpType
ACT = mybir.ActivationFunctionType
AX = mybir.AxisListType

NBATCH, SEQ, DIM = 8, 1024, 128
DEPTH, HEADS, DH, WIN = 2, 8, 64, 64
INNER = HEADS * DH
HID = 341
NPAIR = HEADS // 2
HS = [128, 128, HID - 256]
CH = 256
TPC = CH // 128
WPC = CH // WIN
CPB = SEQ // CH
NCH = NBATCH * CPB
YW = SEQ + 2
NT = NBATCH * SEQ // 128
EPS = 1e-5
ASC = float(1.0 / np.sqrt(np.float32(DIM)))
MASKED = -1e30

C_ID, C_CEN, C_ONE, C_CAU, C_LOC, C_LOC0, C_END = 0, 128, 256, 384, 512, 640, 768


class Queues:

    def __init__(self, nc, ctx):
        self.nc, self.ctx = nc, ctx
        self.items = {e: [] for e in ("tensor", "vector", "scalar", "gpsimd", "sync")}
        self.sems, self.count = {}, {}

    def put(self, engine, fn, waits, sig, inc):
        flat = []
        for w in waits:
            if isinstance(w, (list, tuple)) and not (w and isinstance(w[0], str)):
                flat += [x for x in w if x is not None]
            elif w is not None:
                flat.append(w)
        self.items[engine].append((fn, flat, sig, inc))
        if sig is None:
            return None
        if sig not in self.sems:
            self.sems[sig] = self.ctx.enter_context(self.nc.semaphore(sig))
            self.count[sig] = 0
        self.count[sig] += inc
        return (sig, self.count[sig])

    def pe(self, fn, *waits, sig=None):
        return self.put("tensor", fn, waits, sig, 1)

    def dve(self, fn, *waits, sig=None):
        return self.put("vector", fn, waits, sig, 1)

    def act(self, fn, *waits, sig=None):
        return self.put("scalar", fn, waits, sig, 1)

    def pool(self, fn, *waits, sig=None):
        return self.put("gpsimd", fn, waits, sig, 1)

    def dma(self, fn, *waits, sig=None):
        return self.put("sync", fn, waits, sig, 16)

    def play(self, engine, eng):
        waited = {}
        for fn, waits, sig, inc in self.items[engine]:
            for name, value in waits:
                if waited.get(name, 0) < value:
                    eng.wait_ge(self.sems[name], value)
                    waited[name] = value
            if fn is not None:
                ins = fn(eng)
                if sig is not None:
                    ins.then_inc(self.sems[sig], inc)


def merge(*gens):
    live = [[g, n, 0] for g, n in gens]
    while live:
        live.sort(key=lambda x: (x[2] + 0.5) / x[1])
        item = live[0]
        try:
            next(item[0])
            item[2] += 1
        except StopIteration:
            live.remove(item)


def build_program(nc, a, out, ctx):
    q = Queues(nc, ctx)

    def sb(name, shape, dt=F32):
        return nc.alloc_sbuf_tensor(name, [128] + shape, dt)

    X = sb("X", [NT, 128])
    Y0 = sb("Y0", [NBATCH * YW])
    QB = sb("QB", [2, NPAIR, WPC, 128])
    KT = sb("KT", [2, NPAIR, WIN + CH])
    VP = sb("VP", [2, WPC, INNER])
    OT = sb("OT", [2, NPAIR, CH])
    TAB = sb("TAB", [DEPTH, 4, 8, DH])
    WQKV = sb("WQKV", [DEPTH, 3 * INNER])
    WO = sb("WO", [DEPTH, NPAIR, 128])
    W1 = sb("W1", [DEPTH, 2 * HID])
    W2 = sb("W2", [DEPTH, 3, 128])
    WA = sb("WA", [3, 128])
    CST = sb("CST", [C_END])
    IDB = sb("IDB", [128], BF16)
    MLOC = sb("MLOC", [2, NPAIR, 128], BF16)
    MCAU = sb("MCAU", [128], BF16)
    COLS = sb("COLS", [DEPTH, 16])
    NHALF = sb("NHALF", [16])
    SQ = sb("SQ", [2, INNER])
    T1 = sb("T1", [3, INNER])
    T2 = sb("T2", [2, INNER])
    SS = sb("SS", [2, 16])
    RN = sb("RN", [2, 16])
    P = sb("P", [3, NPAIR, 128])
    PT = sb("PT", [2, NPAIR, 128])
    MX = sb("MX", [3, NPAIR])
    SM = sb("SM", [3, NPAIR])
    RI = sb("RI", [3, NPAIR])
    Y1 = sb("Y1", [2, CH + 2])
    HC = sb("HC", [CH])
    SQL = sb("SQL", [CH])
    RV = sb("RV", [2, 2])
    RB = sb("RB", [TPC, 128])
    HN = sb("HN", [CH])
    G = sb("G", [3, CH])
    H = sb("H", [3, CH])
    YF = sb("YF", [CH])
    ST = sb("ST", [4, 6])
    MV = sb("MV", [4, 2])
    XN = sb("XN", [4, 128])
    PS = nc.alloc_psum_tensor("PS", [128, 8, 512], F32)

    ident = CST[:, C_ID:C_ID + 128]
    center = CST[:, C_CEN:C_CEN + 128]
    ones = CST[:, C_ONE:C_ONE + 1]
    free = [None] * 8

    wreg = VP[:].rearrange("p a b c -> p (a b c)")
    base = wreg[:, 0:4 * 8 * DH].rearrange("p (t m d) -> p t m d", t=4, m=8)
    qk = wreg[:, 2048:2048 + DEPTH * 2 * DH].rearrange("p (l s d) -> p l s d", l=DEPTH, s=2)
    xr = a["L0_attn_x"].rearrange("b (m p) d -> p (b m) d", p=128)
    d_x = [q.dma(lambda e, i=i: e.dma_start(X[:, 8 * i:8 * i + 8, :], xr[:, 8 * i:8 * i + 8, :]), sig=f"load_x{i}")
           for i in range(1)]
    d_c = q.dma(lambda e: e.dma_start(CST[:], a["const"]), sig="load_const")
    q.dma(lambda e: e.dma_start(base, a["table"]), sig="load_scale")
    for l in range(DEPTH):
        for s, n in enumerate(("L0_ffn_q_scale", "L0_ffn_k_scale")):
            d_s = q.dma(lambda e, l=l, s=s, n=n: e.dma_start(qk[:, l, s, :], a[n][l].partition_broadcast(128)),
                        sig="load_scale")
    for l in range(DEPTH):
        q.dma(lambda e, l=l: e.dma_start(WQKV[:, l, :], a["L0_ffn_wqkv"][l]), sig="load_w")
        q.dma(lambda e, l=l: e.dma_start(WO[:, l], a["L0_ffn_wo"][l].rearrange("(n p) m -> p n m", p=128)), sig="load_w")
        q.dma(lambda e, l=l: e.dma_start(W1[:, l, :], a["L0_ffn_w1"][l]), sig="load_w")
        for j in range(3):
            q.dma(lambda e, l=l, j=j: e.dma_start(W2[0:HS[j], l, j, :], a["L0_ffn_w2"][l, 128 * j:128 * j + HS[j], :]),
                  sig="load_w")
            for s in range(2):
                q.dma(lambda e, l=l, j=j, s=s: e.dma_start(
                    COLS[0:HS[j], l, 3 * s + j:3 * s + j + 1],
                    a["L0_ffn_b1"][l, s * HID + 128 * j:s * HID + 128 * j + HS[j]].unsqueeze(1)), sig="load_w")
        for k, n in ((6, "L0_ffn_ln_g"), (7, "L0_ffn_ln_b"), (8, "L0_ffn_b2")):
            q.dma(lambda e, l=l, k=k, n=n: e.dma_start(COLS[:, l, k:k + 1], a[n][l].unsqueeze(1)), sig="load_w")
    for k, n in enumerate(("L0_attn_Wq", "L0_attn_Wk", "L0_attn_Wv")):
        d_w = q.dma(lambda e, k=k, n=n: e.dma_start(WA[:, k, :], a[n]), sig="load_w")
    for i in range(1, 8):
        d_x.append(q.dma(lambda e, i=i: e.dma_start(X[:, 8 * i:8 * i + 8, :], xr[:, 8 * i:8 * i + 8, :]),
                         sig=f"load_x{i}"))

    q.dve(lambda e: e.memset(NHALF[:], -0.5), sig="set")
    q.dve(lambda e: e.memset(QB[:], 0.0), sig="set")
    q.dve(lambda e: e.memset(KT[:], 0.0), sig="set")
    s_set = q.dve(lambda e: e.memset(Y0[64:128, :], 0.0), sig="set")
    q.dve(lambda e: e.tensor_copy(IDB[:], ident), d_c, sig="mask")
    for v, c in ((0, C_LOC), (1, C_LOC0)):
        q.dve(lambda e, v=v, c=c: e.tensor_copy(
            MLOC[:, v], CST[:, c:c + 128].unsqueeze(1).broadcast_to([128, NPAIR, 128])), sig="mask")
    s_mask = q.dve(lambda e: e.tensor_copy(MCAU[:], CST[:, C_CAU:C_CAU + 128]), sig="mask")
    for l in range(DEPTH):
        for t in range(4):
            sc = qk[:, l, t // 2, :].rearrange("p (h d) -> p h d", h=2)
            if t % 2:
                sc = sc[:, ::-1, :]
            sc = sc.unsqueeze(1).broadcast_to([128, 8, 2, 32])
            s_tab = q.dve(lambda e, l=l, t=t, sc=sc: e.tensor_tensor(
                TAB[:, l, t].rearrange("p m (h d) -> p m h d", h=2),
                base[:, t].rearrange("p m (h d) -> p m h d", h=2), sc, ALU.mult), d_s, sig="table")
    b1p = [(l, s, j) for l in range(DEPTH) for s in range(2) for j in range(3)]
    for n, (l, s, j) in enumerate(b1p):
        lo = s * HID + 128 * j
        s_b1m = q.pe(lambda e, l=l, s=s, j=j, lo=lo, n=n: e.matmul(
            PS[0:HS[j], 0, n:n + 1], W1[:, l, lo:lo + HS[j]], COLS[:, l, 7:8], start=True, stop=True),
            d_w, sig="b1_mm")
    for n, (l, s, j) in enumerate(b1p):
        s_b1 = q.dve(lambda e, l=l, s=s, j=j, n=n: e.tensor_tensor(
            COLS[0:HS[j], l, 3 * s + j:3 * s + j + 1], PS[0:HS[j], 0, n:n + 1],
            COLS[0:HS[j], l, 3 * s + j:3 * s + j + 1], ALU.add), s_b1m, d_w, sig="b1_add")
    free[0] = s_b1

    st = {"y0": {}, "x": {}, "qb_free": [s_set, s_set], "kt_free": [s_set, s_set], "vp_free": [s_tab, s_tab],
          "ot_free": [None, None], "y0_read": {}}

    ln = {"n": 0, "xn_free": [None] * 4, "mv_free": [None] * 4}

    def ln_rows(tile):
        k = ln["n"] % 4
        ln["n"] += 1
        w = q.dve(lambda e: e.bn_stats(ST[:, k, :], X[:, tile, :]), st["x"].get(tile), d_x[tile // 8], sig="ln_dve")
        w = q.dve(lambda e: e.bn_aggr(MV[:, k, :], ST[:, k, :]), w, ln["mv_free"][k], sig="ln_dve")
        w = q.dve(lambda e: e.tensor_scalar(MV[:, k, 1:2], MV[:, k, 1:2], EPS, None, ALU.add), w, sig="ln_dve")
        w = q.pool(lambda e: e.tensor_tensor(MV[:, k, 1:2], MV[:, k, 1:2], NHALF[:, 0:1], ALU.pow), w, s_set,
                   sig="ln_rstd")
        w = q.dve(lambda e: e.tensor_scalar(XN[:, k, :], X[:, tile, :], MV[:, k, 0:1], MV[:, k, 1:2],
                                            ALU.subtract, ALU.mult), w, ln["xn_free"][k], sig="ln_dve")
        ln["mv_free"][k] = w
        return k, w

    def ln_turn(k, w, bank, slot):
        w = q.pe(lambda e: e.transpose(PS[:, bank, slot * 128:slot * 128 + 128], XN[:, k, :], ident),
                 w, d_c, free[bank], sig="ln_turn")
        ln["xn_free"][k] = w
        return w

    def stage_i(c):
        rows = []
        for i in range(TPC):
            rows.append(ln_rows(c * TPC + i))
            yield
        bank = abank()
        for i in range(TPC):
            w = ln_turn(*rows[i], bank, i)
        col = (c // CPB) * YW + (c % CPB) * CH
        w1 = q.act(lambda e: e.copy(Y0[0:64, col:col + CH], PS[0:64, bank, 0:CH]), w, s_set, sig="y0_low")
        w2 = q.dve(lambda e: e.tensor_copy(Y0[64:128, col + 1:col + 1 + CH], PS[64:128, bank, 0:CH]), w, s_set,
                   sig="y0_high")
        st["y0"][c] = (w1, w2)
        free[bank] = (w1, w2)
        yield

    aring = {"n": 0, "sq": [None] * 2, "t1": [None] * 3, "t2": [None] * 2, "rn": [None] * 2, "k": 0}

    def abank():
        b = aring["n"] % 3
        aring["n"] += 1
        return b

    def stage_a(l, c):
        s = c % 2
        col = (c // CPB) * YW + (c % CPB) * CH
        first = c % CPB == 0
        ready = []
        for n in (c, c - 1):
            if n >= 0:
                ready += st["y0"][n]
        kt_w, qb_w, vp_w = [], [], []
        prev_k = st.get("kt_w")
        if first:
            if l >= 0:
                kt_w.append(q.pool(lambda e: e.memset(KT[:, s, :, 0:WIN], 0.0), st["kt_free"][s], s_set, sig="k_head"))
        else:
            kt_w.append(q.pool(lambda e: e.tensor_copy(KT[:, s, :, 0:WIN], KT[:, 1 - s, :, CH:CH + WIN]),
                               st["kt_free"][s], *prev_k, sig="k_head"))
        def tile(i):
            m = (c % CPB) * TPC + i
            hT = Y0[:, col + 128 * i:col + 128 * i + 128]
            r = aring["k"] % 2
            aring["k"] += 1
            t1s, banks, sums = {}, {}, []
            for x in range(2):
                b = banks[x] = abank()
                pj = q.pe(lambda e, b=b, x=x: e.matmul(PS[:, b, :], hT, WQKV[:, l, x * INNER:(x + 1) * INNER],
                                                       start=True, stop=True), free[b], *ready, d_w, sig="proj")
                k = aring.setdefault("nsq", 0) % 2
                aring["nsq"] += 1
                w = q.act(lambda e, b=b, k=k: e.activation(SQ[:, k, :], PS[:, b, :], ACT.Square),
                          pj, aring["sq"][k], sig="square")
                squared = w
                w = q.dve(lambda e, k=k, x=x: e.tensor_reduce(
                    SS[:, r, 8 * x:8 * x + 8], SQ[:, k, :].rearrange("p (h d) -> p h d", h=HEADS), AX.X, ALU.add),
                    w, aring["rn"][r], sig="sumsq")
                aring["sq"][k] = w
                sums.append(w)
                k = aring.setdefault("nt", 0) % 3
                k2 = aring["nt"] % 2
                aring["nt"] += 1
                tc = TAB[:, l, 2 * x, m, :].unsqueeze(1).broadcast_to([128, HEADS, DH])
                ts = TAB[:, l, 2 * x + 1, m, :].rearrange("p (t d) -> p t d", t=2).unsqueeze(1).broadcast_to(
                    [128, HEADS, 2, 32])
                w1 = q.dve(lambda e, b=b, k=k, tc=tc: e.tensor_tensor(
                    T1[:, k, :].rearrange("p (h d) -> p h d", h=HEADS),
                    PS[:, b, :].rearrange("p (h d) -> p h d", h=HEADS), tc, ALU.mult),
                    pj, squared, s_tab, aring["t1"][k], sig="rot_cos")
                w2 = q.dve(lambda e, b=b, k=k2, ts=ts: e.tensor_tensor(
                    T2[:, k, :].rearrange("p (h t d) -> p h t d", h=HEADS, t=2),
                    PS[:, b, :].rearrange("p (h t d) -> p h t d", h=HEADS, t=2)[:, :, ::-1, :], ts, ALU.mult),
                    pj, s_tab, aring["t2"][k2], sig="rot_sin")
                free[b] = w2
                w = q.pool(lambda e, k=k, k2=k2: e.tensor_tensor(T1[:, k, :], T1[:, k, :], T2[:, k2, :], ALU.add),
                           w1, w2, sig="rot_add")
                aring["t2"][k2] = w
                t1s[x] = (k, w)
                yield
            b = abank()
            pj = q.pe(lambda e, b=b: e.matmul(PS[:, b, :], hT, WQKV[:, l, 2 * INNER:], start=True, stop=True),
                      free[b], sig="proj")
            if i == TPC - 1:
                st["y0_read"][c] = pj
            wv = q.act(lambda e, b=b, i=i: e.copy(VP[:, s, 2 * i + 1, :], PS[:, b, :]),
                       pj, st["vp_free"][s], st.get(("vp_dma", s)), sig="v_copy")
            free[b] = wv
            vp_w.append(wv)
            w = q.dve(lambda e, r=r: e.tensor_scalar(SS[:, r, :], SS[:, r, :], 1e-24, None, ALU.max), *sums,
                      sig="norm_max")
            w = q.pool(lambda e, r=r: e.tensor_tensor(RN[:, r, :], SS[:, r, :], NHALF[:], ALU.pow), w, s_set,
                       sig="norm_pow")
            aring["rn"][r] = w
            for x in range(2):
                k, wt = t1s[x]
                t1s[x] = (k, q.pool(lambda e, k=k, x=x, r=r: e.tensor_tensor(
                    T1[:, k, :].rearrange("p (h d) -> p h d", h=HEADS),
                    T1[:, k, :].rearrange("p (h d) -> p h d", h=HEADS),
                    RN[:, r, 8 * x:8 * x + 8].unsqueeze(2).broadcast_to([128, HEADS, DH]), ALU.mult), wt, w,
                    sig="norm_mul"))
            yield
            for x in range(2):
                k, wt = t1s[x]
                b = abank()
                for p in range(NPAIR):
                    tr = q.pe(lambda e, b=b, p=p, k=k: e.transpose(
                        PS[:, b, 128 * p:128 * p + 128], T1[:, k, 128 * p:128 * p + 128], ident),
                        free[b], wt, d_c, sig="qk_turn")
                aring["t1"][k] = tr
                src = PS[:, b, :].rearrange("p (n w i) -> p n w i", n=NPAIR, w=2)
                if x == 0:
                    wa = q.act(lambda e, src=src, i=i: e.copy(QB[0:64, s, :, 2 * i:2 * i + 2, 0:64], src[0:64]),
                               tr, st["qb_free"][s], sig="q_even")
                    wd = q.dve(lambda e, src=src, i=i: e.tensor_copy(QB[64:128, s, :, 2 * i:2 * i + 2, 64:128],
                                                                     src[64:128]), tr, st["qb_free"][s], sig="q_odd")
                    qb_w.extend([wa, wd])
                    free[b] = (wa, wd)
                else:
                    wk = q.act(lambda e, b=b, i=i: e.copy(
                        KT[:, s, :, WIN + 128 * i:WIN + 128 * i + 128],
                        PS[:, b, :].rearrange("p (n t) -> p n t", n=NPAIR)), tr, st["kt_free"][s], s_set, sig="k_copy")
                    kt_w.append(wk)
                    free[b] = wk
                yield
        for i in range(TPC):
            yield from tile(i)
        d1 = q.dma(lambda e: e.dma_start(VP[64:128, s, 0::2, :], VP[0:64, s, 1::2, :]), *vp_w, sig="v_shift")
        d2 = q.dma(lambda e: e.dma_start(VP[0:64, s, 2::2, :], VP[64:128, s, 1:WPC - 1:2, :]), sig="v_shift")
        if first:
            w = q.pool(lambda e: e.memset(VP[0:64, s, 0, :], 0.0), st["vp_free"][s], st.get(("vp_dma", s)),
                       sig="v_zero")
            st[("vp_dma", 1 - s)] = None
        else:
            w = None
            d2 = q.dma(lambda e: e.dma_start(VP[0:64, s, 0, :], VP[64:128, 1 - s, WPC - 1, :]), sig="v_shift")
            st[("vp_dma", 1 - s)] = d2
        st["kt_w"] = kt_w
        st[("a", c)] = (kt_w + qb_w + vp_w + [d2, w])
        yield

    bring = {"n": 0, "g": 0, "p": [None] * 3, "pt": [None] * 2, "bank": [3, 4, 5]}

    def bbank():
        b = 3 + bring["n"] % 3
        bring["n"] += 1
        return b

    def stage_b(c):
        s = c % 2
        ready = st[("a", c)]
        ot_w = []

        def scores(w):
            g = bring["g"] % 3
            bring["g"] += 1
            b = bbank()
            v = 1 if (c % CPB == 0 and w == 0) else 0
            q.pe(lambda e: e.matmul(PS[:, b, :], IDB[:], MLOC[:, v].rearrange("p n k -> p (n k)"), start=True,
                                    stop=True), free[b], s_mask)
            for p in range(NPAIR):
                mm = q.pe(lambda e, p=p: e.matmul(PS[:, b, 128 * p:128 * p + 128], QB[:, s, p, w, :],
                                                  KT[:, s, p, w * WIN:w * WIN + 128], start=False,
                                                  stop=True, skip_group_check=True), *ready, sig="scores")
            mx = q.dve(lambda e: e.tensor_reduce(MX[:, g, :], PS[:, b, :].rearrange("p (n k) -> p n k", n=NPAIR),
                                                 AX.X, ALU.max, negate=True), mm, bring["p"][g], sig="row_max")
            for p in range(NPAIR):
                ex = q.act(lambda e, p=p: e.activation(P[:, g, p, :], PS[:, b, 128 * p:128 * p + 128], ACT.Exp,
                                                       bias=MX[:, g, p:p + 1], accum_out=SM[:, g, p:p + 1]),
                           mx, bring["p"][g], sig="exp")
            free[b] = ex
            ri = q.dve(lambda e: e.reciprocal(RI[:, g, :], SM[:, g, :]), ex, sig="row_inv")
            sc = q.pool(lambda e: e.tensor_tensor(P[:, g], P[:, g],
                                                  RI[:, g, :].unsqueeze(2).broadcast_to([128, NPAIR, 128]),
                                                  ALU.mult), ri, sig="p_scale")
            return g, sc

        def values(w, g, sc):
            k = w % 2
            b = bbank()
            for p in range(NPAIR):
                tr = q.pe(lambda e, p=p: e.transpose(PS[:, b, 128 * p:128 * p + 128], P[:, g, p, :], ident),
                          free[b], sc, sig="p_turn")
            bring["p"][g] = tr
            cp = q.dve(lambda e: e.tensor_copy(PT[:, k].rearrange("p n k -> p (n k)"), PS[:, b, :]), tr,
                       bring["pt"][k], sig="p_copy")
            free[b] = cp
            yield
            b2 = bbank()
            for p in range(NPAIR):
                pv = q.pe(lambda e, p=p: e.matmul(PS[:, b2, 128 * p:128 * p + 128],
                                                       VP[:, s, w, 128 * p:128 * p + 128], PT[:, k, p, :],
                                                       start=True, stop=True), free[b2], cp, sig="pv")
            bring["pt"][k] = pv
            src = PS[:, b2, :].rearrange("p (n k) -> p n k", n=NPAIR)
            o1 = q.act(lambda e: e.copy(OT[0:64, s, :, WIN * w:WIN * w + WIN], src[0:64, :, 0:64]), pv,
                       st["ot_free"][s], sig="o_even")
            o2 = q.dve(lambda e: e.tensor_copy(OT[64:128, s, :, WIN * w:WIN * w + WIN], src[64:128, :, 64:128]), pv,
                       st["ot_free"][s], sig="o_odd")
            ot_w.extend([o1, o2])
            free[b2] = (o1, o2)
            st["pv"] = pv
            yield

        nxt = scores(0)
        yield
        for w in range(WPC):
            cur = nxt
            if w + 1 < WPC:
                nxt = scores(w + 1)
                yield
            yield from values(w, *cur)
        st["qb_free"][s] = st["kt_free"][s] = st["vp_free"][s] = st["pv"]
        st[("b", c)] = ot_w[-2:]

    cr = {"y1": [None] * 2}

    def stage_c(l, c, last):
        s = c % 2
        col = (c // CPB) * YW + (c % CPB) * CH
        first = c % CPB == 0
        for p in range(NPAIR):
            mm = q.pe(lambda e, p=p: e.matmul(PS[:, 6, 0:CH], WO[:, l, p, :], OT[:, s, p, :], start=(p == 0),
                                              stop=(p == NPAIR - 1)), free[6], *st[("b", c)], sig="wo")
        st["ot_free"][s] = mm
        yd = list(st["y0"][c])
        if first:
            h = q.dve(lambda e: e.memset(Y1[64:128, s, 0:1], 0.0), cr["y1"][s], sig="y1_head")
        else:
            h = q.dve(lambda e: e.tensor_copy(Y1[64:128, s, 0:1], Y1[64:128, 1 - s, CH:CH + 1]), cr["y1"][s],
                       cr["y1_w"], sig="y1_head")
        q.dve(lambda e: e.tensor_tensor(Y1[0:64, s, 0:CH], PS[0:64, 6, 0:CH], Y0[0:64, col:col + CH], ALU.add),
              mm, *yd, cr["y1"][s], sig="y1")
        y1 = q.dve(lambda e: e.tensor_tensor(Y1[64:128, s, 1:CH + 1], PS[64:128, 6, 0:CH],
                                             Y0[64:128, col + 1:col + 1 + CH], ALU.add), mm, sig="y1")
        cr["y1_w"] = y1
        free[6] = y1
        yield
        ce = q.pe(lambda e: e.matmul(PS[:, 7, 0:CH], center, Y1[:, s, 0:CH], start=True, stop=True), free[7], y1, h,
                  sig="center")
        w = q.act(lambda e: e.activation(SQL[:], PS[:, 7, 0:CH], ACT.Square), ce, cr.get("sql"), sig="sq_c")
        yield
        for i in range(TPC):
            v = q.pe(lambda e, i=i: e.matmul(PS[:, 6, i:i + 1], SQL[:, 128 * i:128 * i + 128], ones, start=True,
                                             stop=True), w, free[6], sig="var")
        cr["sql"] = v
        w = q.dve(lambda e: e.tensor_scalar(RV[:, 0, :], PS[:, 6, 0:TPC], EPS, None, ALU.add), v, cr.get("rv"),
                  sig="var_eps")
        free[6] = w
        w = q.pool(lambda e: e.tensor_tensor(RV[:, 1, :], RV[:, 0, :], NHALF[:, 0:TPC], ALU.pow), w, sig="rstd")
        cr["rv"] = w
        rb = q.pool(lambda e: e.tensor_copy(RB[:], RV[:, 1, :].unsqueeze(2).broadcast_to([128, TPC, 128])), w,
                    cr.get("rb"), sig="rstd_row")
        yield
        for i in range(TPC):
            bc = q.pe(lambda e, i=i: e.matmul(PS[:, 6, 128 * i:128 * i + 128], RB[:, i, :], ident, start=True,
                                              stop=True), rb, free[6], sig="rstd_all")
        cr["rb"] = bc
        w = q.act(lambda e: e.copy(HC[:], PS[:, 6, 0:CH]), bc, cr.get("hc"), sig="rstd_copy")
        free[6] = w
        hn = q.dve(lambda e: e.scalar_tensor_tensor(HN[:], PS[:, 7, 0:CH], COLS[:, l, 6:7], HC[:], ALU.mult,
                                                    ALU.mult), w, cr.get("hn"), sig="hn")
        cr["hc"] = hn
        free[7] = hn
        yield

        def up(bank, off, part, j, *w):
            lo = part * HID + 128 * j
            return q.pe(lambda e: e.matmul(PS[0:HS[j], bank, off:off + CH], W1[:, l, lo:lo + HS[j]], HN[:],
                                           start=True, stop=True), hn, free[bank], *w, sig="w1")

        up(6, 0, 1, 0)
        g1 = up(6, CH, 1, 1)
        up(7, 0, 1, 2)
        g2 = up(7, CH, 0, 2)
        yield
        for j, (bank, off, w) in enumerate(((6, 0, g1), (6, CH, g1), (7, 0, g2))):
            ge = q.act(lambda e, j=j, bank=bank, off=off: e.activation(
                G[0:HS[j], j, :], PS[0:HS[j], bank, off:off + CH], ACT.Gelu, bias=COLS[0:HS[j], l, 3 + j:4 + j]),
                w, s_b1, cr.get("g"), sig="gelu")
        free[6] = ge
        yield
        up(6, 0, 0, 0)
        a1 = up(6, CH, 0, 1)
        cr["hn"] = a1
        for j, (bank, off, w) in enumerate(((6, 0, a1), (6, CH, a1), (7, CH, g2))):
            hw = q.dve(lambda e, j=j, bank=bank, off=off: e.scalar_tensor_tensor(
                H[0:HS[j], j, :], PS[0:HS[j], bank, off:off + CH], COLS[0:HS[j], l, j:j + 1], G[0:HS[j], j, :],
                ALU.add, ALU.mult), w, ge, cr.get("h"), sig="glu")
        cr["g"] = hw
        free[6] = free[7] = hw
        yield
        for j in range(3):
            mm = q.pe(lambda e, j=j: e.matmul(PS[:, 7, 0:CH], W2[0:HS[j], l, j, :], H[0:HS[j], j, :],
                                              start=(j == 0), stop=(j == 2)), hw, free[7], sig="w2")
        cr["h"] = mm
        b2 = COLS[:, l, 8:9]
        if not last:
            rd = [st["y0_read"].get(c + 1), st["y0_read"].get(c)] if c + 1 < NCH else [st["y0_read"].get(c)]
            q.dve(lambda e: e.scalar_tensor_tensor(Y0[0:64, col:col + CH], PS[0:64, 7, 0:CH], b2[0:64],
                                                   Y1[0:64, s, 0:CH], ALU.add, ALU.add), mm, *rd, sig="y0_new")
            y = q.dve(lambda e: e.scalar_tensor_tensor(Y0[64:128, col + 1:col + 1 + CH], PS[64:128, 7, 0:CH],
                                                       b2[64:128], Y1[64:128, s, 1:CH + 1], ALU.add, ALU.add),
                      mm, cr["y1_w"], sig="y0_new")
            st["y0"][c] = (y,)
            st["y0n"] = y
            cr["y1"][s] = y
            free[7] = y
            yield
            return
        q.dve(lambda e: e.scalar_tensor_tensor(YF[0:64, :], PS[0:64, 7, 0:CH], b2[0:64], Y1[0:64, s, 0:CH],
                                               ALU.add, ALU.add), mm, cr.get("yf"), sig="y_last")
        y = q.dve(lambda e: e.scalar_tensor_tensor(YF[64:128, :], PS[64:128, 7, 0:CH], b2[64:128],
                                                   Y1[64:128, s, 1:CH + 1], ALU.add, ALU.add), mm, cr["y1_w"],
                  sig="y_last")
        cr["y1"][s] = y
        free[7] = y
        yield
        for i in range(TPC):
            t = q.pe(lambda e, i=i: e.transpose(PS[:, 6, 128 * i:128 * i + 128], YF[:, 128 * i:128 * i + 128],
                                                ident), y, free[6], sig="y_turn")
        cr["yf"] = t
        xs = X[:, c * TPC:(c + 1) * TPC, :]
        x = q.dve(lambda e: e.scalar_tensor_tensor(xs, PS[:, 6, 0:CH].rearrange("p (t d) -> p t d", t=TPC), 0.5, xs,
                                                   ALU.mult, ALU.add), t, sig="x_new")
        free[6] = x
        for i in range(TPC):
            st["x"][c * TPC + i] = x
        yield

    def ffn(final):
        def seq(gs):
            for g in gs:
                yield from g

        steps = [(l, c) for l in range(DEPTH) for c in range(NCH)]
        for c in range(2):
            merge((stage_i(c), 3))
        n = len(steps)
        for t in range(n + 2):
            gens = []
            if t < n:
                gens.append((stage_a(*steps[t]), 5 * TPC + 1))
            if 1 <= t <= n:
                gens.append((stage_b(steps[t - 1][1]), 4 * WPC))
            if t >= 2:
                l, c = steps[t - 2]
                gens.append((stage_c(l, c, l == DEPTH - 1), 10))
            if t + 2 < NCH:
                gens.append((stage_i(t + 2), 3))
            merge(*gens)
            if final and t >= 2 and steps[t - 2][0] == DEPTH - 1 and (steps[t - 2][1] + 1) % CPB == 0:
                b = steps[t - 2][1] // CPB
                q.dma(lambda e, b=b: e.dma_start(outr[:, 8 * b:8 * b + 8, :], X[:, 8 * b:8 * b + 8, :]),
                      st["x"][8 * b + 7], sig="store")

    outr = out.rearrange("b (m p) d -> p (b m) d", p=128)

    big = QB[:].rearrange("p a b c d -> p (a b c d)")
    HT = [Y0[:, 0:SEQ], Y0[:, SEQ:2 * SEQ]]
    QT = [Y0[:, 2 * SEQ:3 * SEQ], Y0[:, 3 * SEQ:4 * SEQ]]
    KF = [Y0[:, 4 * SEQ:5 * SEQ], Y0[:, 5 * SEQ:6 * SEQ]]
    VF = [Y0[:, 6 * SEQ:7 * SEQ], Y0[:, 7 * SEQ:8 * SEQ]]
    PF = [big[:, k * SEQ:(k + 1) * SEQ] for k in range(2)]
    PTF = [big[:, (2 + k) * SEQ:(3 + k) * SEQ] for k in range(2)]
    mm_ = {"s": [None] * 2, "p": [None] * 2, "pt": [None] * 2, "n": 0, "pb": 0}

    def att_in(b):
        s = b % 2
        for h in range(2):
            for i in range(4):
                w = ln_turn(*ln_rows(8 * b + 4 * h + i), 6, i)
                yield
            ht = q.act(lambda e, h=h: e.copy(HT[s][:, 512 * h:512 * h + 512], PS[:, 6, :]), w, mm_["s"][s],
                       sig="ht")
            free[6] = ht
            for x, dst in ((0, QT), (1, KF)):
                p = q.pe(lambda e, h=h, x=x: e.matmul(PS[:, 7, :], WA[:, x, :], HT[s][:, 512 * h:512 * h + 512],
                                                      start=True, stop=True), ht, free[7], d_w, sig="att_proj")
                free[7] = q.act(lambda e, h=h, dst=dst: e.copy(dst[s][:, 512 * h:512 * h + 512], PS[:, 7, :]), p,
                                mm_["s"][s], sig="att_qkv")
                yield
            for i in range(4):
                p = q.pe(lambda e, h=h, i=i: e.matmul(PS[:, 7, 128 * i:128 * i + 128],
                                                      HT[s][:, 512 * h + 128 * i:512 * h + 128 * i + 128],
                                                      WA[:, 2, :], start=True, stop=True), free[7], sig="att_proj")
            w = free[7] = q.act(lambda e, h=h: e.copy(VF[s][:, 512 * h:512 * h + 512], PS[:, 7, :]), p, mm_["s"][s],
                                sig="att_qkv")
            yield
        st[("m", b)] = w

    def att(b):
        s = b % 2
        ready = st[("m", b)]

        def scores(i):
            k = mm_["n"] % 2
            mm_["n"] += 1
            nk = 128 * (i + 1)
            for o in range(0, nk, 512):
                bank = 2 * k + o // 512
                n = min(512, nk - o)
                diag = o + n == nk
                if diag:
                    q.pe(lambda e, n=n, bank=bank: e.matmul(PS[:, bank, n - 128:n], IDB[:], MCAU[:], start=True,
                                                            stop=True), s_mask, free[bank])
                mm = q.pe(lambda e, o=o, n=n, bank=bank, diag=diag: e.matmul(
                    PS[:, bank, 0:n], QT[s][:, 128 * i:128 * i + 128], KF[s][:, o:o + n], start=not diag,
                    stop=True, skip_group_check=True), ready, free[bank], sig="att_s")
            src = PS[:, 2 * k:2 * k + 2, :].rearrange("p b k -> p (b k)")[:, 0:nk]
            mx = q.dve(lambda e: e.tensor_reduce(MX[:, k, 0:1], src, AX.X, ALU.max, negate=True), mm, mm_["p"][k],
                       sig="att_max")
            mx = q.dve(lambda e: e.tensor_scalar(MX[:, k, 1:2], MX[:, k, 0:1], ASC, None, ALU.mult), mx,
                       sig="att_max")
            ex = q.act(lambda e: e.activation(PF[k][:, 0:nk], src, ACT.Exp, bias=MX[:, k, 1:2], scale=ASC,
                                              accum_out=SM[:, k, 0:1]), mx, mm_["p"][k], sig="att_exp")
            free[2 * k] = free[2 * k + 1] = ex
            ri = q.dve(lambda e: e.reciprocal(RI[:, k, 0:1], SM[:, k, 0:1]), ex, mm_.get(("ri", k)), sig="att_inv")
            return k, ex, ri

        def values(i, k, ex, ri):
            for o in range(0, i + 1, 4):
                n = min(4, i + 1 - o)
                for j in range(n):
                    tr = q.pe(lambda e, o=o, j=j: e.transpose(PS[:, 4, 128 * j:128 * j + 128],
                                                              PF[k][:, 128 * (o + j):128 * (o + j) + 128], ident),
                              ex, free[4], sig="att_turn")
                free[4] = q.dve(lambda e, o=o, n=n: e.tensor_copy(PTF[k][:, 128 * o:128 * (o + n)],
                                                                  PS[:, 4, 0:128 * n]), tr, mm_["pt"][k],
                                sig="att_pt")
                yield
            mm_["p"][k] = tr
            cp = free[4]
            for j in range(i + 1):
                pv = q.pe(lambda e, j=j: e.matmul(PS[:, 5, 0:128], PTF[k][:, 128 * j:128 * j + 128],
                                                  VF[s][:, 128 * j:128 * j + 128], start=(j == 0), stop=(j == i)),
                          cp, free[5], sig="att_pv")
            mm_["pt"][k] = pv
            t = 8 * b + i
            x = q.dve(lambda e: e.scalar_tensor_tensor(X[:, t, :], PS[:, 5, 0:128], RI[:, k, 0:1], X[:, t, :],
                                                       ALU.mult, ALU.add), pv, ri, sig="att_x")
            free[5] = x
            mm_[("ri", k)] = x
            st["x"][t] = x
            yield
            mm_["s"][s] = pv

        nxt = scores(0)
        yield
        for i in range(8):
            cur = nxt
            if i + 1 < 8:
                nxt = scores(i + 1)
                yield
            yield from values(i, *cur)

    def barrier(*names):
        for e in ("tensor", "vector", "scalar", "gpsimd", "sync"):
            q.put(e, None, [(n, q.count[n]) for n in names], None, 1)

    ffn(False)
    barrier("x_new", "y_turn", "pv", "w2")
    merge((att_in(0), 14))
    for b in range(NBATCH):
        gens = [(att(b), 28)]
        if b + 1 < NBATCH:
            gens.append((att_in(b + 1), 14))
        merge(*gens)
    barrier("att_x", "att_pv", "att_turn", "att_proj")
    s1 = q.dve(lambda e: e.memset(QB[:], 0.0), sig="set2")
    s2 = q.dve(lambda e: e.memset(Y0[64:128, :], 0.0), sig="set2")
    barrier("set2")
    ffn(True)
    q.dma(None, ("store", q.count["store"]))

    block = ctx.enter_context(nc.Block())

    @block.sync
    def _(e):
        q.play("sync", e)

    @block.scalar
    def _(e):
        q.play("scalar", e)

    @block.vector
    def _(e):
        q.play("vector", e)

    @block.gpsimd
    def _(e):
        q.play("gpsimd", e)

    @block.tensor
    def _(e):
        q.play("tensor", e)


_INS = ['L0_attn_x', 'L0_attn_Wk', 'L0_attn_Wq', 'L0_attn_Wv', 'L0_ffn_wqkv', 'L0_ffn_q_scale', 'L0_ffn_k_scale',
        'L0_ffn_wo', 'L0_ffn_ln_g', 'L0_ffn_ln_b', 'L0_ffn_w1', 'L0_ffn_b1', 'L0_ffn_w2', 'L0_ffn_b2']


def _tables():
    f = np.float32
    half = np.arange(0, DH, 2, dtype=f)
    inv = (f(1.0) / (f(10000.0) ** (half / f(DH)))).astype(f)
    t = np.arange(SEQ, dtype=f)
    fr = t[:, None] * inv[None, :]
    fr = np.concatenate([fr, fr], -1)
    bs = ((half + f(0.4 * DH)) / f(1.4 * DH)).astype(f)
    pw = ((t - f(SEQ // 2)) / f(WIN // 2)).astype(f)
    sc = (bs[None, :] ** pw[:, None]).astype(f)
    sc = np.concatenate([sc, sc], -1)
    cos, sin = np.cos(fr).astype(f), np.sin(fr).astype(f)
    sg = np.where(np.arange(DH) < DH // 2, f(-1), f(1))[None, :]
    tabs = [f(8) * cos * sc, f(8) * sin * sc * sg, cos / sc, sin / sc * sg]
    tabs = np.stack(tabs).astype(f).reshape(4, 8, 128, DH)
    return np.ascontiguousarray(tabs.transpose(2, 0, 1, 3))


def _consts():
    c = np.zeros((128, C_END), np.float32)
    p = np.arange(128)
    c[:, C_ID:C_ID + 128] = np.eye(128)
    c[:, C_CEN:C_CEN + 128] = np.eye(128) - 1.0 / 128
    c[:, C_ONE:C_ONE + 128] = 1.0 / 128
    c[:, C_CAU:C_CAU + 128] = np.where(p[None, :] <= p[:, None], 0.0, MASKED)
    i = (p % 64)[:, None]
    ok = (p[None, :] >= i) & (p[None, :] <= i + 64)
    c[:, C_LOC:C_LOC + 128] = np.where(ok, 0.0, MASKED)
    c[:, C_LOC0:C_LOC0 + 128] = np.where(ok & (p[None, :] >= 64), 0.0, MASKED)
    return c


def kernel(**inputs):
    from contextlib import ExitStack
    import concourse.bacc as _bacc
    from concourse.bass_utils import run_bass_kernel_spmd as _run

    nc = _bacc.Bacc("TRN2", target_bir_lowering=False, num_devices=1)
    arrays, args = {}, {}
    feeds = {n: np.ascontiguousarray(inputs[n]) for n in _INS}
    feeds["table"], feeds["const"] = _tables(), _consts()
    for name, v in feeds.items():
        arrays[f"in_{name}_dram"] = v
        args[name] = nc.dram_tensor(f"in_{name}_dram", v.shape, mybir.dt.from_np(v.dtype), kind="ExternalInput").ap()
    out = nc.dram_tensor("out_0_dram", (NBATCH, SEQ, DIM), F32, kind="ExternalOutput").ap()
    with ExitStack() as ctx:
        build_program(nc, args, out, ctx)
    r = _run(nc, [arrays], core_ids=[0])
    return r.results[0]["out_0_dram"]
```

```python
import numpy as np
import concourse.bass as bass
from concourse import mybir

F32 = mybir.dt.float32
BF16 = mybir.dt.bfloat16
ALU = mybir.AluOpType
ACT = mybir.ActivationFunctionType
AX = mybir.AxisListType

NBATCH, SEQ, DIM = 8, 1024, 128
DEPTH, HEADS, DH, WIN = 2, 8, 64, 64
INNER = HEADS * DH
HID = 341
NPAIR = HEADS // 2
HS = [128, 128, HID - 256]
CH = 256
TPC = CH // 128
WPC = CH // WIN
CPB = SEQ // CH
NCH = NBATCH * CPB
YW = SEQ + 2
NT = NBATCH * SEQ // 128
EPS = 1e-5
ASC = float(1.0 / np.sqrt(np.float32(DIM)))
MASKED = -1e30

SPAN = dict(proj=858, exp=265, pv=214, rot_add=1225, norm_mul=1001, p_scale=1001, scores=214, w1=427, sumsq=602,
            rot_cos=602, rot_sin=602, row_max=598, p_copy=598, qk_turn=107, square=478, p_turn=107, wo=427, o_odd=331,
            w2=427, q_odd=598, glu=396, gelu=358, o_even=264, rstd_row=973, v_copy=478, q_even=478, k_copy=478,
            ln_dve=138, att_pv=214, att_s=858, ln_rstd=464, y1=335, rstd=628, att_proj=500, center=427, hn=396,
            y0_new=396, y_last=396, row_inv=94, att_exp=800, att_pt=531, att_turn=107, sq_c=264, rstd_copy=264,
            ln_turn=107, att_qkv=478, x_new=335, y0_high=331, y_turn=107, y0_low=264, att_x=263, norm_pow=1470,
            k_head=700, v_shift=1800, store=1000, norm_max=77, rstd_all=214, ht=478, att_max=600, v_zero=462)
LATE = dict(tensor=150, vector=80, scalar=150, gpsimd=80, sync=300)

C_ID, C_CEN, C_ONE, C_CAU, C_LOC, C_LOC0, C_END = 0, 128, 256, 384, 512, 640, 768


class Queues:

    def __init__(self, nc, ctx):
        self.nc, self.ctx = nc, ctx
        self.items = {e: [] for e in ("tensor", "vector", "scalar", "gpsimd", "sync")}
        self.sems, self.count = {}, {}
        self.clock = {e: 0.0 for e in self.items}
        self.due = {}
        self.table = None

    def when(self, *tokens):
        return max([self.due.get(t, 0.0) for t in flat(tokens)], default=0.0)

    def put(self, engine, fn, waits, sig, inc):
        waits = flat(waits)
        self.items[engine].append((fn, waits, sig, inc))
        start = max(self.clock[engine], self.when(waits))
        if sig in ("gelu", "exp", "att_exp") and (self.table == "gelu") != (sig == "gelu"):
            start += 1300
            self.table = sig
        self.clock[engine] = start + SPAN.get(sig, 100)
        if sig is None:
            return None
        if sig not in self.sems:
            self.sems[sig] = self.ctx.enter_context(self.nc.semaphore(sig))
            self.count[sig] = 0
        self.count[sig] += inc
        self.due[(sig, self.count[sig])] = self.clock[engine] + LATE[engine]
        if engine == "sync":
            self.clock[engine] = start + 100
        return (sig, self.count[sig])

    def pe(self, fn, *waits, sig=None):
        return self.put("tensor", fn, waits, sig, 1)

    def dve(self, fn, *waits, sig=None):
        return self.put("vector", fn, waits, sig, 1)

    def act(self, fn, *waits, sig=None):
        return self.put("scalar", fn, waits, sig, 1)

    def pool(self, fn, *waits, sig=None):
        return self.put("gpsimd", fn, waits, sig, 1)

    def dma(self, fn, *waits, sig=None):
        return self.put("sync", fn, waits, sig, 16)

    def play(self, engine, eng):
        waited = {}
        for fn, waits, sig, inc in self.items[engine]:
            for name, value in waits:
                if waited.get(name, 0) < value:
                    eng.wait_ge(self.sems[name], value)
                    waited[name] = value
            if fn is not None:
                ins = fn(eng)
                if sig is not None:
                    ins.then_inc(self.sems[sig], inc)


def flat(tokens):
    out = []
    for t in tokens:
        if t is None:
            continue
        if isinstance(t, tuple) and t and isinstance(t[0], str):
            out.append(t)
        else:
            out += flat(t)
    return out


class Slots:

    def __init__(self, q, places, tokens=None):
        self.q, self.open = q, {p: tokens for p in places}

    def best(self):
        return min(self.open, key=lambda p: self.q.when(self.open[p]), default=None)

    def take(self):
        p = self.best()
        return p, self.open.pop(p)

    def give(self, p, *tokens):
        self.open[p] = list(tokens)


def run_tasks(q, kinds):
    todo = [list(reversed(tasks)) for tasks, _ in kinds]
    live = []
    while True:
        for k, (_, most) in enumerate(kinds):
            while todo[k] and sum(x[0] == k for x in live) < most:
                rank, gen = todo[k].pop()
                live.append([k, rank, gen, next(gen)])
        if not live:
            return
        best = None
        for item in live:
            engine, tokens, slots = item[3]
            if callable(tokens):
                tokens = tokens()
                if tokens is None:
                    continue
                item[3] = (engine, tokens, slots)
            if any(not s.open for s in slots):
                continue
            at = max([q.clock[engine], q.when(tokens)] + [q.when(s.open[s.best()]) for s in slots])
            if best is None or (at, item[1]) < best[0]:
                best = ((at, item[1]), item)
        if best is None:
            raise RuntimeError("no task can go on")
        item = best[1]
        try:
            item[3] = next(item[2])
        except StopIteration:
            live.remove(item)


def build_program(nc, a, out, ctx):
    q = Queues(nc, ctx)

    def sb(name, shape, dt=F32):
        return nc.alloc_sbuf_tensor(name, [128] + shape, dt)

    X = sb("X", [NT, 128])
    Y0 = sb("Y0", [NBATCH * YW])
    QB = sb("QB", [2, NPAIR, WPC, 128])
    KT = sb("KT", [2, NPAIR, WIN + CH])
    VP = sb("VP", [2, WPC, INNER])
    OT = sb("OT", [2, NPAIR, CH])
    TAB = sb("TAB", [DEPTH, 4, 8, DH])
    WQKV = sb("WQKV", [DEPTH, 3 * INNER])
    WO = sb("WO", [DEPTH, NPAIR, 128])
    W1 = sb("W1", [DEPTH, 2 * HID])
    W2 = sb("W2", [DEPTH, 3, 128])
    WA = sb("WA", [3, 128])
    CST = sb("CST", [C_END])
    IDB = sb("IDB", [128], BF16)
    MLOC = sb("MLOC", [2, NPAIR, 128], BF16)
    MCAU = sb("MCAU", [128], BF16)
    COLS = sb("COLS", [DEPTH, 16])
    NHALF = sb("NHALF", [16])
    SQ = sb("SQ", [2, INNER])
    T1 = sb("T1", [4, INNER])
    T2 = sb("T2", [2, INNER])
    SS = sb("SS", [4, 8])
    RN = sb("RN", [4, 8])
    P = sb("P", [3, NPAIR, 128])
    PT = sb("PT", [2, NPAIR, 128])
    MX = sb("MX", [3, NPAIR])
    SM = sb("SM", [3, NPAIR])
    RI = sb("RI", [3, NPAIR])
    Y1 = sb("Y1", [2, CH + 2])
    SQL = sb("SQL", [2, CH])
    RV = sb("RV", [2, 2, 2])
    RB = sb("RB", [2, TPC, 128])
    HN = sb("HN", [2, CH])
    G = sb("G", [2, 3, CH])
    ST = sb("ST", [4, 6])
    MV = sb("MV", [4, 2])
    XN = sb("XN", [4, 128])
    AM = sb("AM", [4, 4])
    PS = nc.alloc_psum_tensor("PS", [128, 8, 512], F32)

    ident = CST[:, C_ID:C_ID + 128]
    center = CST[:, C_CEN:C_CEN + 128]
    ones = CST[:, C_ONE:C_ONE + 1]

    wreg = VP[:].rearrange("p a b c -> p (a b c)")
    base = wreg[:, 0:4 * 8 * DH].rearrange("p (t m d) -> p t m d", t=4, m=8)
    qk = wreg[:, 2048:2048 + DEPTH * 2 * DH].rearrange("p (l s d) -> p l s d", l=DEPTH, s=2)
    xr = a["L0_attn_x"].rearrange("b (m p) d -> p (b m) d", p=128)
    d_x = [q.dma(lambda e, i=i: e.dma_start(X[:, 8 * i:8 * i + 8, :], xr[:, 8 * i:8 * i + 8, :]), sig=f"load_x{i}")
           for i in range(1)]
    d_c = q.dma(lambda e: e.dma_start(CST[:], a["const"]), sig="load_const")
    q.dma(lambda e: e.dma_start(base, a["table"]), sig="load_scale")
    for l in range(DEPTH):
        for s, n in enumerate(("L0_ffn_q_scale", "L0_ffn_k_scale")):
            d_s = q.dma(lambda e, l=l, s=s, n=n: e.dma_start(qk[:, l, s, :], a[n][l].partition_broadcast(128)),
                        sig="load_scale")
    for l in range(DEPTH):
        q.dma(lambda e, l=l: e.dma_start(WQKV[:, l, :], a["L0_ffn_wqkv"][l]), sig="load_w")
        q.dma(lambda e, l=l: e.dma_start(WO[:, l], a["L0_ffn_wo"][l].rearrange("(n p) m -> p n m", p=128)), sig="load_w")
        q.dma(lambda e, l=l: e.dma_start(W1[:, l, :], a["L0_ffn_w1"][l]), sig="load_w")
        for j in range(3):
            q.dma(lambda e, l=l, j=j: e.dma_start(W2[0:HS[j], l, j, :], a["L0_ffn_w2"][l, 128 * j:128 * j + HS[j], :]),
                  sig="load_w")
            for s in range(2):
                q.dma(lambda e, l=l, j=j, s=s: e.dma_start(
                    COLS[0:HS[j], l, 3 * s + j:3 * s + j + 1],
                    a["L0_ffn_b1"][l, s * HID + 128 * j:s * HID + 128 * j + HS[j]].unsqueeze(1)), sig="load_w")
        for k, n in ((6, "L0_ffn_ln_g"), (7, "L0_ffn_ln_b"), (8, "L0_ffn_b2")):
            q.dma(lambda e, l=l, k=k, n=n: e.dma_start(COLS[:, l, k:k + 1], a[n][l].unsqueeze(1)), sig="load_w")
    for k, n in enumerate(("L0_attn_Wq", "L0_attn_Wk", "L0_attn_Wv")):
        d_w = q.dma(lambda e, k=k, n=n: e.dma_start(WA[:, k, :], a[n]), sig="load_w")
    for i in range(1, 8):
        d_x.append(q.dma(lambda e, i=i: e.dma_start(X[:, 8 * i:8 * i + 8, :], xr[:, 8 * i:8 * i + 8, :]),
                         sig=f"load_x{i}"))

    q.dve(lambda e: e.memset(NHALF[:], -0.5), sig="set")
    q.dve(lambda e: e.memset(QB[:], 0.0), sig="set")
    q.dve(lambda e: e.memset(KT[:], 0.0), sig="set")
    s_set = q.dve(lambda e: e.memset(Y0[64:128, :], 0.0), sig="set")
    q.dve(lambda e: e.tensor_copy(IDB[:], ident), d_c, sig="mask")
    for v, c in ((0, C_LOC), (1, C_LOC0)):
        q.dve(lambda e, v=v, c=c: e.tensor_copy(
            MLOC[:, v], CST[:, c:c + 128].unsqueeze(1).broadcast_to([128, NPAIR, 128])), sig="mask")
    s_mask = q.dve(lambda e: e.tensor_copy(MCAU[:], CST[:, C_CAU:C_CAU + 128]), sig="mask")
    for l in range(DEPTH):
        for t in range(4):
            sc = qk[:, l, t // 2, :].rearrange("p (h d) -> p h d", h=2)
            if t % 2:
                sc = sc[:, ::-1, :]
            sc = sc.unsqueeze(1).broadcast_to([128, 8, 2, 32])
            s_tab = q.dve(lambda e, l=l, t=t, sc=sc: e.tensor_tensor(
                TAB[:, l, t].rearrange("p m (h d) -> p m h d", h=2),
                base[:, t].rearrange("p m (h d) -> p m h d", h=2), sc, ALU.mult), d_s, sig="table")
    b1p = [(l, s, j) for l in range(DEPTH) for s in range(2) for j in range(3)]
    for n, (l, s, j) in enumerate(b1p):
        lo = s * HID + 128 * j
        s_b1m = q.pe(lambda e, l=l, s=s, j=j, lo=lo, n=n: e.matmul(
            PS[0:HS[j], 0, n:n + 1], W1[:, l, lo:lo + HS[j]], COLS[:, l, 7:8], start=True, stop=True),
            d_w, sig="b1_mm")
    for n, (l, s, j) in enumerate(b1p):
        s_b1 = q.dve(lambda e, l=l, s=s, j=j, n=n: e.tensor_tensor(
            COLS[0:HS[j], l, 3 * s + j:3 * s + j + 1], PS[0:HS[j], 0, n:n + 1],
            COLS[0:HS[j], l, 3 * s + j:3 * s + j + 1], ALU.add), s_b1m, d_w, sig="b1_add")

    banks = Slots(q, range(1, 8))
    banks.give(0, s_b1)
    t1_slots = Slots(q, range(4))
    t2_slots, sq_slots = Slots(q, range(2)), Slots(q, range(2))
    ss_slots = Slots(q, range(4))
    p_slots, pt_slots = Slots(q, range(3)), Slots(q, range(2))
    xn_slots = Slots(q, range(4))
    c_slots = Slots(q, range(2))
    st = {}

    def all_of(*keys):
        def get():
            out = []
            for k in keys:
                if k not in st:
                    return None
                out.append(st[k])
            return out
        return get

    def ln_rows(tile):
        yield "vector", [d_x[tile // 8], st.get(("x", tile))], [xn_slots]
        k, gone = xn_slots.take()
        w = q.dve(lambda e: e.bn_stats(ST[:, k, :], X[:, tile, :]), st.get(("x", tile)), d_x[tile // 8],
                  sig="ln_dve")
        w = q.dve(lambda e: e.bn_aggr(MV[:, k, :], ST[:, k, :]), w, gone, sig="ln_dve")
        w = q.dve(lambda e: e.tensor_scalar(MV[:, k, 1:2], MV[:, k, 1:2], EPS, None, ALU.add), w, sig="ln_dve")
        yield "gpsimd", [w], []
        w = q.pool(lambda e: e.tensor_tensor(MV[:, k, 1:2], MV[:, k, 1:2], NHALF[:, 0:1], ALU.pow), w, s_set,
                   sig="ln_rstd")
        yield "vector", [w], []
        w = q.dve(lambda e: e.tensor_scalar(XN[:, k, :], X[:, tile, :], MV[:, k, 0:1], MV[:, k, 1:2],
                                            ALU.subtract, ALU.mult), w, gone, sig="ln_dve")
        return k, w

    def ln_turn(rows, bank, gone):
        for i, (k, w) in enumerate(rows):
            t = q.pe(lambda e, i=i, k=k: e.transpose(PS[:, bank, i * 128:i * 128 + 128], XN[:, k, :], ident),
                     w, d_c, gone, sig="ln_turn")
            xn_slots.give(k, t)
        return t

    def stage_i(c):
        rows = []
        for i in range(TPC):
            rows.append((yield from ln_rows(c * TPC + i)))
        yield "tensor", [w for _, w in rows], [banks]
        bank, gone = banks.take()
        t = ln_turn(rows, bank, gone)
        col = (c // CPB) * YW + (c % CPB) * CH
        yield "scalar", [t], []
        w1 = q.act(lambda e: e.copy(Y0[0:64, col:col + CH], PS[0:64, bank, 0:CH]), t, s_set, sig="y0_low")
        yield "vector", [t], []
        w2 = q.dve(lambda e: e.tensor_copy(Y0[64:128, col + 1:col + 1 + CH], PS[64:128, bank, 0:CH]), t, s_set,
                   sig="y0_high")
        st[("y0", 0, c)] = (w1, w2)
        banks.give(bank, w1, w2)

    def y0_ready(l, c):
        return all_of(*[("y0", l, n) for n in ([c] if c % CPB == 0 else [c, c - 1])])

    def y0_was_read(l, c, token):
        n, _ = st.get(("y0_reads", l, c), (0, None))
        st[("y0_reads", l, c)] = (n + 1, token)
        if n + 1 == 3 * TPC:
            st[("y0_read", l, c)] = token

    def old(name, t):
        return all_of((name, t - 2)) if t >= 2 else (lambda: [])

    def stage_qk(l, c, i, x):
        t = l * NCH + c
        s = t % 2
        m = (c % CPB) * TPC + i
        col = (c // CPB) * YW + (c % CPB) * CH + 128 * i
        first = c % CPB == 0
        ready = y0_ready(l, c)
        yield "tensor", ready, [banks]
        b, gone = banks.take()
        pj = q.pe(lambda e: e.matmul(PS[:, b, :], Y0[:, col:col + 128], WQKV[:, l, x * INNER:(x + 1) * INNER],
                                     start=True, stop=True), gone, ready(), d_w, sig="proj")
        y0_was_read(l, c, pj)
        yield "scalar", [pj], [sq_slots]
        k, gone = sq_slots.take()
        sq = q.act(lambda e: e.activation(SQ[:, k, :], PS[:, b, :], ACT.Square), pj, gone, sig="square")
        yield "vector", [sq], [ss_slots]
        r, gone = ss_slots.take()
        w = q.dve(lambda e: e.tensor_reduce(SS[:, r, :], SQ[:, k, :].rearrange("p (h d) -> p h d", h=HEADS), AX.X,
                                            ALU.add), sq, gone, sig="sumsq")
        sq_slots.give(k, w)
        yield "vector", [sq], [t1_slots]
        k1, gone = t1_slots.take()
        tc = TAB[:, l, 2 * x, m, :].unsqueeze(1).broadcast_to([128, HEADS, DH])
        ts = TAB[:, l, 2 * x + 1, m, :].rearrange("p (t d) -> p t d", t=2).unsqueeze(1).broadcast_to(
            [128, HEADS, 2, 32])
        w1 = q.dve(lambda e: e.tensor_tensor(
            T1[:, k1, :].rearrange("p (h d) -> p h d", h=HEADS),
            PS[:, b, :].rearrange("p (h d) -> p h d", h=HEADS), tc, ALU.mult), sq, s_tab, gone, sig="rot_cos")
        mx = q.dve(lambda e: e.tensor_scalar(SS[:, r, :], SS[:, r, :], 1e-24, None, ALU.max), w, sig="norm_max")
        yield "vector", [sq], [t2_slots]
        k2, gone = t2_slots.take()
        w2 = q.dve(lambda e: e.tensor_tensor(
            T2[:, k2, :].rearrange("p (h t d) -> p h t d", h=HEADS, t=2),
            PS[:, b, :].rearrange("p (h t d) -> p h t d", h=HEADS, t=2)[:, :, ::-1, :], ts, ALU.mult),
            sq, s_tab, gone, sig="rot_sin")
        banks.give(b, w2)
        yield "gpsimd", [mx], []
        pw = q.pool(lambda e: e.tensor_tensor(RN[:, r, :], SS[:, r, :], NHALF[:, 0:8], ALU.pow), mx, s_set,
                    sig="norm_pow")
        yield "gpsimd", [w1, w2], []
        ad = q.pool(lambda e: e.tensor_tensor(T1[:, k1, :], T1[:, k1, :], T2[:, k2, :], ALU.add), w1, w2,
                    sig="rot_add")
        t2_slots.give(k2, ad)
        yield "gpsimd", [ad, pw], []
        nm = q.pool(lambda e: e.tensor_tensor(
            T1[:, k1, :].rearrange("p (h d) -> p h d", h=HEADS), T1[:, k1, :].rearrange("p (h d) -> p h d", h=HEADS),
            RN[:, r, :].unsqueeze(2).broadcast_to([128, HEADS, DH]), ALU.mult), ad, pw, sig="norm_mul")
        ss_slots.give(r, nm)
        yield "tensor", [nm], [banks]
        b2, gone = banks.take()
        for p in range(NPAIR):
            tr = q.pe(lambda e, p=p: e.transpose(PS[:, b2, 128 * p:128 * p + 128],
                                                 T1[:, k1, 128 * p:128 * p + 128], ident), gone, nm, d_c,
                      sig="qk_turn")
        t1_slots.give(k1, tr)
        src = PS[:, b2, :].rearrange("p (n w i) -> p n w i", n=NPAIR, w=2)
        was = old("scored", t)
        if x == 0:
            yield "scalar", was, []
            wa = q.act(lambda e: e.copy(QB[0:64, s, :, 2 * i:2 * i + 2, 0:64], src[0:64]), tr, was(), s_set,
                       sig="q_even")
            yield "vector", [tr], []
            wd = q.dve(lambda e: e.tensor_copy(QB[64:128, s, :, 2 * i:2 * i + 2, 64:128], src[64:128]), tr, was(),
                       s_set, sig="q_odd")
            st[("q", t, i)] = (wa, wd)
            banks.give(b2, wa, wd)
            return
        if i == TPC - 1 and t >= 1 and (t - 1) % CPB != 0:
            was = all_of(("scored", t - 2), ("k_head", t - 1)) if t >= 2 else all_of(("k_head", t - 1))
        yield "scalar", was, []
        yield "scalar", [tr], []
        wk = q.act(lambda e: e.copy(KT[:, s, :, WIN + 128 * i:WIN + 128 * i + 128],
                                    PS[:, b2, :].rearrange("p (n t) -> p n t", n=NPAIR)), tr, was(), s_set,
                   sig="k_copy")
        st[("k", t, i)] = wk
        banks.give(b2, wk)

    def stage_head(l, c):
        t = l * NCH + c
        s = t % 2
        was = old("scored", t)
        yield "gpsimd", was, []
        if c % CPB == 0:
            w = q.pool(lambda e: e.memset(KT[:, s, :, 0:WIN], 0.0), was(), s_set, sig="k_head")
        else:
            before = all_of(("k", t - 1, TPC - 1))
            yield "gpsimd", before, []
            w = q.pool(lambda e: e.tensor_copy(KT[:, s, :, 0:WIN], KT[:, 1 - s, :, CH:CH + WIN]), was(), before(),
                       sig="k_head")
        st[("k_head", t)] = w

    def stage_v(l, c, i):
        t = l * NCH + c
        s = t % 2
        col = (c // CPB) * YW + (c % CPB) * CH + 128 * i
        first = c % CPB == 0
        ready = y0_ready(l, c)
        yield "tensor", ready, [banks]
        b, gone = banks.take()
        pj = q.pe(lambda e: e.matmul(PS[:, b, :], Y0[:, col:col + 128], WQKV[:, l, 2 * INNER:], start=True,
                                     stop=True), gone, ready(), d_w, sig="proj")
        y0_was_read(l, c, pj)
        was = [("valued", t - 2)] if t >= 2 else []
        if i == TPC - 1 and t >= 1 and (t - 1) % CPB != 0:
            was.append(("v_shifted", t - 1, 0))
        was = all_of(*was)
        yield "scalar", was, []
        yield "scalar", [pj], []
        wv = q.act(lambda e: e.copy(VP[:, s, 2 * i + 1, :], PS[:, b, :]), pj, was(), s_tab, sig="v_copy")
        st[("v", t, i)] = wv
        banks.give(b, wv)
        sem = f"v_shift{s}{i}"
        d = q.dma(lambda e: e.dma_start(VP[64:128, s, 2 * i, :], VP[0:64, s, 2 * i + 1, :]), wv, was(), s_tab,
                  sig=sem)
        z = None
        if i > 0:
            before = all_of(("v", t, i - 1))
            yield "sync", before, []
            d = q.dma(lambda e: e.dma_start(VP[0:64, s, 2 * i, :], VP[64:128, s, 2 * i - 1, :]), before(), sig=sem)
        elif first:
            yield "gpsimd", [], []
            z = q.pool(lambda e: e.memset(VP[0:64, s, 0, :], 0.0), was(), s_tab, sig="v_zero")
        else:
            before = all_of(("v", t - 1, TPC - 1))
            yield "sync", before, []
            d = q.dma(lambda e: e.dma_start(VP[0:64, s, 0, :], VP[64:128, 1 - s, WPC - 1, :]), before(), sig=sem)
        st[("v_shifted", t, i)] = (d, z)

    def stage_b(l, c, w):
        t = l * NCH + c
        s = t % 2
        i = w // 2
        ready = all_of(("q", t, i), ("k_head", t), *[("k", t, n) for n in range(i + 1)])
        yield "tensor", ready, [banks, p_slots]
        b, gone = banks.take()
        g, gone_p = p_slots.take()
        v = 1 if (c % CPB == 0 and w == 0) else 0
        q.pe(lambda e: e.matmul(PS[:, b, :], IDB[:], MLOC[:, v].rearrange("p n k -> p (n k)"), start=True,
                                stop=True), gone, s_mask)
        for p in range(NPAIR):
            mm = q.pe(lambda e, p=p: e.matmul(PS[:, b, 128 * p:128 * p + 128], QB[:, s, p, w, :],
                                              KT[:, s, p, w * WIN:w * WIN + 128], start=False,
                                              stop=True, skip_group_check=True), ready(), sig="scores")
        done(("scored", t), mm)
        yield "vector", [mm], []
        mx = q.dve(lambda e: e.tensor_reduce(MX[:, g, :], PS[:, b, :].rearrange("p (n k) -> p n k", n=NPAIR),
                                             AX.X, ALU.max, negate=True), mm, gone_p, sig="row_max")
        yield "scalar", [mx], []
        for p in range(NPAIR):
            ex = q.act(lambda e, p=p: e.activation(P[:, g, p, :], PS[:, b, 128 * p:128 * p + 128], ACT.Exp,
                                                   bias=MX[:, g, p:p + 1], accum_out=SM[:, g, p:p + 1]),
                       mx, gone_p, sig="exp")
        banks.give(b, ex)
        yield "vector", [ex], []
        ri = q.dve(lambda e: e.reciprocal(RI[:, g, :], SM[:, g, :]), ex, sig="row_inv")
        yield "gpsimd", [ri], []
        sc = q.pool(lambda e: e.tensor_tensor(P[:, g], P[:, g], RI[:, g, :].unsqueeze(2).broadcast_to(
            [128, NPAIR, 128]), ALU.mult), ri, sig="p_scale")
        yield "tensor", [sc], [banks, pt_slots]
        b2, gone = banks.take()
        k, gone_t = pt_slots.take()
        for p in range(NPAIR):
            tr = q.pe(lambda e, p=p: e.transpose(PS[:, b2, 128 * p:128 * p + 128], P[:, g, p, :], ident),
                      gone, sc, sig="p_turn")
        p_slots.give(g, tr)
        yield "vector", [tr], []
        cp = q.dve(lambda e: e.tensor_copy(PT[:, k].rearrange("p n k -> p (n k)"), PS[:, b2, :]), tr, gone_t,
                   sig="p_copy")
        banks.give(b2, cp)
        vals = all_of(("v", t, i)) if w % 2 else all_of(("v_shifted", t, i))
        yield "tensor", vals, []
        yield "tensor", [cp], [banks]
        b3, gone = banks.take()
        for p in range(NPAIR):
            pv = q.pe(lambda e, p=p: e.matmul(PS[:, b3, 128 * p:128 * p + 128], VP[:, s, w, 128 * p:128 * p + 128],
                                              PT[:, k, p, :], start=True, stop=True), gone, cp, vals(), sig="pv")
        pt_slots.give(k, pv)
        done(("valued", t), pv)
        src = PS[:, b3, :].rearrange("p (n k) -> p n k", n=NPAIR)
        was = old("wo", t)
        yield "scalar", was, []
        yield "scalar", [pv], []
        o1 = q.act(lambda e: e.copy(OT[0:64, s, :, WIN * w:WIN * w + WIN], src[0:64, :, 0:64]), pv, was(),
                   sig="o_even")
        yield "vector", [pv], []
        o2 = q.dve(lambda e: e.tensor_copy(OT[64:128, s, :, WIN * w:WIN * w + WIN], src[64:128, :, 64:128]), pv,
                   was(), sig="o_odd")
        banks.give(b3, o1, o2)
        done(("windows", t), (o1, o2))

    def done(key, token):
        got = st.setdefault(("some", key), [])
        got.append(token)
        if len(got) == WPC:
            st[key] = got

    def stage_c(l, c, final):
        t = l * NCH + c
        s = t % 2
        col = (c // CPB) * YW + (c % CPB) * CH
        last = l == DEPTH - 1
        ready = all_of(("windows", t))
        yield "tensor", ready, [banks, c_slots]
        z, gone_c = c_slots.take()
        b, gone = banks.take()
        for p in range(NPAIR):
            mm = q.pe(lambda e, p=p: e.matmul(PS[:, b, 0:CH], WO[:, l, p, :], OT[:, s, p, :], start=(p == 0),
                                              stop=(p == NPAIR - 1)), gone, ready(), sig="wo")
        st[("wo", t)] = mm
        y0 = st[("y0", l, c)]
        was = []
        if c % CPB:
            was.append(("y1", t - 1))
        if t >= 2:
            was.append(("y1_free", t - 2))
        if t >= 1 and (t - 1) % CPB:
            was.append(("y1", t - 1))
        was = all_of(*was)
        yield "vector", was, []
        yield "vector", [mm], []
        if c % CPB == 0:
            h = q.dve(lambda e: e.memset(Y1[64:128, s, 0:1], 0.0), was(), sig="y1_head")
        else:
            h = q.dve(lambda e: e.tensor_copy(Y1[64:128, s, 0:1], Y1[64:128, 1 - s, CH:CH + 1]), was(),
                      sig="y1_head")
        q.dve(lambda e: e.tensor_tensor(Y1[0:64, s, 0:CH], PS[0:64, b, 0:CH], Y0[0:64, col:col + CH], ALU.add),
              mm, y0, was(), sig="y1")
        y1 = q.dve(lambda e: e.tensor_tensor(Y1[64:128, s, 1:CH + 1], PS[64:128, b, 0:CH],
                                             Y0[64:128, col + 1:col + 1 + CH], ALU.add), mm, y0, was(), sig="y1")
        st[("y1", t)] = (h, y1)
        banks.give(b, y1)
        yield "tensor", [y1, h], [banks]
        bc, gone = banks.take()
        ce = q.pe(lambda e: e.matmul(PS[:, bc, 0:CH], center, Y1[:, s, 0:CH], start=True, stop=True), gone, y1, h,
                  sig="center")
        yield "scalar", [ce], []
        sq = q.act(lambda e: e.activation(SQL[:, z], PS[:, bc, 0:CH], ACT.Square), ce, gone_c, sig="sq_c")
        yield "tensor", [sq], [banks]
        bv, gone = banks.take()
        for i in range(TPC):
            v = q.pe(lambda e, i=i: e.matmul(PS[:, bv, i:i + 1], SQL[:, z, 128 * i:128 * i + 128], ones,
                                             start=True, stop=True), sq, gone, sig="var")
        yield "vector", [v], []
        w = q.dve(lambda e: e.tensor_scalar(RV[:, z, 0, :], PS[:, bv, 0:TPC], EPS, None, ALU.add), v, gone_c,
                  sig="var_eps")
        banks.give(bv, w)
        yield "gpsimd", [w], []
        w = q.pool(lambda e: e.tensor_tensor(RV[:, z, 1, :], RV[:, z, 0, :], NHALF[:, 0:TPC], ALU.pow), w,
                   sig="rstd")
        rb = q.pool(lambda e: e.tensor_copy(RB[:, z], RV[:, z, 1, :].unsqueeze(2).broadcast_to([128, TPC, 128])), w,
                    gone_c, sig="rstd_row")
        yield "tensor", [rb], [banks]
        br, gone = banks.take()
        for i in range(TPC):
            al = q.pe(lambda e, i=i: e.matmul(PS[:, br, 128 * i:128 * i + 128], RB[:, z, i, :], ident, start=True,
                                              stop=True), rb, gone, sig="rstd_all")
        yield "scalar", [al], []
        w = q.act(lambda e: e.copy(SQL[:, z], PS[:, br, 0:CH]), al, v, sig="rstd_copy")
        banks.give(br, w)
        yield "vector", [w], []
        hn = q.dve(lambda e: e.scalar_tensor_tensor(HN[:, z], PS[:, bc, 0:CH], COLS[:, l, 6:7], SQL[:, z], ALU.mult,
                                                    ALU.mult), w, gone_c, sig="hn")
        banks.give(bc, hn)

        def up(bank, off, part, j, gone):
            lo = part * HID + 128 * j
            return q.pe(lambda e: e.matmul(PS[0:HS[j], bank, off:off + CH], W1[:, l, lo:lo + HS[j]], HN[:, z],
                                           start=True, stop=True), hn, gone, sig="w1")

        yield "tensor", [hn], [banks]
        b6, gone = banks.take()
        up(b6, 0, 1, 0, gone)
        g1 = up(b6, CH, 1, 1, gone)
        yield "tensor", [hn], [banks]
        b7, gone = banks.take()
        up(b7, 0, 1, 2, gone)
        g2 = up(b7, CH, 0, 2, gone)
        yield "scalar", [g2], []
        for j, (bank, off, w) in enumerate(((b6, 0, g1), (b6, CH, g1), (b7, 0, g2))):
            ge = q.act(lambda e, j=j, bank=bank, off=off: e.activation(
                G[0:HS[j], z, j, :], PS[0:HS[j], bank, off:off + CH], ACT.Gelu, bias=COLS[0:HS[j], l, 3 + j:4 + j]),
                w, s_b1, gone_c, sig="gelu")
        yield "tensor", [ge], []
        up(b6, 0, 0, 0, ge)
        a1 = up(b6, CH, 0, 1, ge)
        yield "vector", [a1], []
        for j, (bank, off, w) in enumerate(((b6, 0, a1), (b6, CH, a1), (b7, CH, g2))):
            hw = q.dve(lambda e, j=j, bank=bank, off=off: e.scalar_tensor_tensor(
                G[0:HS[j], z, j, :], PS[0:HS[j], bank, off:off + CH], COLS[0:HS[j], l, j:j + 1], G[0:HS[j], z, j, :],
                ALU.add, ALU.mult), w, ge, gone_c, sig="glu")
        banks.give(b6, hw)
        banks.give(b7, hw)
        yield "tensor", [hw], [banks]
        bw, gone = banks.take()
        for j in range(3):
            mm = q.pe(lambda e, j=j: e.matmul(PS[:, bw, 0:CH], W2[0:HS[j], l, j, :], G[0:HS[j], z, j, :],
                                              start=(j == 0), stop=(j == 2)), hw, gone, sig="w2")
        b2 = COLS[:, l, 8:9]
        if not last:
            reads = [("y0_read", l, c)] + ([("y0_read", l, c + 1)] if (c + 1) % CPB else [])
            reads = all_of(*reads)
            yield "vector", reads, []
            yield "vector", [mm], []
            q.dve(lambda e: e.scalar_tensor_tensor(Y0[0:64, col:col + CH], PS[0:64, bw, 0:CH], b2[0:64],
                                                   Y1[0:64, s, 0:CH], ALU.add, ALU.add), mm, reads(), y1,
                  sig="y0_new")
            y = q.dve(lambda e: e.scalar_tensor_tensor(Y0[64:128, col + 1:col + 1 + CH], PS[64:128, bw, 0:CH],
                                                       b2[64:128], Y1[64:128, s, 1:CH + 1], ALU.add, ALU.add),
                      mm, y1, sig="y0_new")
            st[("y0", l + 1, c)] = y
            st[("y1_free", t)] = y
            banks.give(bw, y)
            c_slots.give(z, y, mm)
            return
        yield "vector", [mm], []
        q.dve(lambda e: e.scalar_tensor_tensor(HN[0:64, z], PS[0:64, bw, 0:CH], b2[0:64], Y1[0:64, s, 0:CH],
                                               ALU.add, ALU.add), mm, y1, gone_c, sig="y_last")
        y = q.dve(lambda e: e.scalar_tensor_tensor(HN[64:128, z], PS[64:128, bw, 0:CH], b2[64:128],
                                                   Y1[64:128, s, 1:CH + 1], ALU.add, ALU.add), mm, y1, gone_c,
                  sig="y_last")
        st[("y1_free", t)] = y
        banks.give(bw, y)
        yield "tensor", [y], [banks]
        bt, gone = banks.take()
        for i in range(TPC):
            tr = q.pe(lambda e, i=i: e.transpose(PS[:, bt, 128 * i:128 * i + 128], HN[:, z, 128 * i:128 * i + 128],
                                                 ident), y, gone, sig="y_turn")
        yield "vector", [tr], []
        xs = X[:, c * TPC:(c + 1) * TPC, :]
        x = q.dve(lambda e: e.scalar_tensor_tensor(xs, PS[:, bt, 0:CH].rearrange("p (t d) -> p t d", t=TPC), 0.5, xs,
                                                   ALU.mult, ALU.add), tr, sig="x_new")
        banks.give(bt, x)
        c_slots.give(z, x, mm)
        for i in range(TPC):
            st[("x", c * TPC + i)] = x
        if final:
            q.dma(lambda e: e.dma_start(outr[:, TPC * c:TPC * (c + 1), :], X[:, TPC * c:TPC * (c + 1), :]), x,
                  sig="store")

    outr = out.rearrange("b (m p) d -> p (b m) d", p=128)

    def forget(*names):
        for k in list(st):
            if k[0] in names or k[0] == "some":
                del st[k]

    def ffn(final):
        steps = [(l, c) for l in range(DEPTH) for c in range(NCH)]
        run_tasks(q, [
            ([(l * NCH + c + 2, stage_c(l, c, final)) for l, c in steps], 2),
            ([(l * NCH + c + 1 + w / WPC, stage_b(l, c, w)) for l, c in steps for w in range(WPC)], 3),
            ([(l * NCH + c, stage_head(l, c)) for l, c in steps], 1),
            ([(l * NCH + c + i / TPC, stage_qk(l, c, i, x)) for l, c in steps for i in range(TPC)
              for x in (1, 0)], 4),
            ([(l * NCH + c + i / TPC, stage_v(l, c, i)) for l, c in steps for i in range(TPC)], 2),
            ([(c - 1, stage_i(c)) for c in range(NCH)], 1),
        ])
        forget("y0", "y0_reads", "y0_read", "scored", "valued", "windows", "q", "k", "v", "k_head", "v_shifted",
               "wo", "y1", "y1_free")

    bigq = QB[:].rearrange("p a b c d -> p (a b c d)")
    bigv = VP[:].rearrange("p a b c -> p (a b c)")
    HT = [Y0[:, 0:SEQ], Y0[:, SEQ:2 * SEQ]]
    QT = [Y0[:, 2 * SEQ:3 * SEQ], Y0[:, 3 * SEQ:4 * SEQ]]
    KF = [Y0[:, 4 * SEQ:5 * SEQ], Y0[:, 5 * SEQ:6 * SEQ]]
    VF = [Y0[:, 6 * SEQ:7 * SEQ], Y0[:, 7 * SEQ:8 * SEQ]]
    PF = [bigq[:, k * SEQ:(k + 1) * SEQ] for k in range(4)]
    PTF = [bigv[:, k * SEQ:(k + 1) * SEQ] for k in range(4)]

    def att_in(b, h, banks_):
        s = b % 2
        was = (lambda: []) if b < 2 else all_of(("att_done", b - 2))
        yield "vector", was, []
        rows = []
        for i in range(4):
            rows.append((yield from ln_rows(8 * b + 4 * h + i)))
        yield "tensor", [w for _, w in rows], [banks_]
        bk, gone = banks_.take()
        t = ln_turn(rows, bk, gone)
        yield "scalar", [t], []
        ht = q.act(lambda e: e.copy(HT[s][:, 512 * h:512 * h + 512], PS[:, bk, :]), t, was(), sig="ht")
        banks_.give(bk, ht)
        got = []
        for x, dst in ((0, QT), (1, KF), (2, VF)):
            yield "tensor", [ht], [banks_]
            bx, gone = banks_.take()
            if x < 2:
                p = q.pe(lambda e, bx=bx, x=x: e.matmul(PS[:, bx, :], WA[:, x, :], HT[s][:, 512 * h:512 * h + 512],
                                                        start=True, stop=True), ht, gone, d_w, sig="att_proj")
            else:
                for i in range(4):
                    p = q.pe(lambda e, bx=bx, i=i: e.matmul(
                        PS[:, bx, 128 * i:128 * i + 128], HT[s][:, 512 * h + 128 * i:512 * h + 128 * i + 128],
                        WA[:, 2, :], start=True, stop=True), ht, gone, d_w, sig="att_proj")
            yield "scalar", [p], []
            w = q.act(lambda e, bx=bx, dst=dst: e.copy(dst[s][:, 512 * h:512 * h + 512], PS[:, bx, :]), p, was(),
                      sig="att_qkv")
            banks_.give(bx, w)
            got.append(w)
        st[("att_in", b, h)] = got

    def att(b, i, banks_, pairs, pf, ptf):
        s = b % 2
        nk = 128 * (i + 1)
        ready = all_of(*[("att_in", b, h) for h in range(i // 4 + 1)])
        yield "tensor", ready, [pairs, pf]
        (ba, bb), gone = pairs.take()
        k, gone_p = pf.take()
        for o in range(0, nk, 512):
            bank = ba if o == 0 else bb
            n = min(512, nk - o)
            diag = o + n == nk
            if diag:
                q.pe(lambda e, n=n, bank=bank: e.matmul(PS[:, bank, n - 128:n], IDB[:], MCAU[:], start=True,
                                                        stop=True), s_mask, gone)
            mm = q.pe(lambda e, o=o, n=n, bank=bank, diag=diag: e.matmul(
                PS[:, bank, 0:n], QT[s][:, 128 * i:128 * i + 128], KF[s][:, o:o + n], start=not diag,
                stop=True, skip_group_check=True), ready(), gone, sig="att_s")
        src = PS[:, ba:ba + 2, :].rearrange("p b k -> p (b k)")[:, 0:nk]
        yield "vector", [mm], []
        mx = q.dve(lambda e: e.tensor_reduce(AM[:, k, 0:1], src, AX.X, ALU.max, negate=True), mm, gone_p,
                   sig="att_max")
        mx = q.dve(lambda e: e.tensor_scalar(AM[:, k, 1:2], AM[:, k, 0:1], ASC, None, ALU.mult), mx, sig="att_bias")
        yield "scalar", [mx], []
        ex = q.act(lambda e: e.activation(PF[k][:, 0:nk], src, ACT.Exp, bias=AM[:, k, 1:2], scale=ASC,
                                          accum_out=AM[:, k, 2:3]), mx, gone_p, sig="att_exp")
        pairs.give((ba, bb), ex)
        yield "vector", [ex], []
        ri = q.dve(lambda e: e.reciprocal(AM[:, k, 3:4], AM[:, k, 2:3]), ex, sig="att_inv")
        cps = []
        for o in range(0, i + 1, 4):
            n = min(4, i + 1 - o)
            yield "tensor", [ex], [banks_] + ([ptf] if o == 0 else [])
            bt, gone = banks_.take()
            if o == 0:
                kt, gone_t = ptf.take()
            for j in range(n):
                tr = q.pe(lambda e, o=o, j=j, bt=bt: e.transpose(
                    PS[:, bt, 128 * j:128 * j + 128], PF[k][:, 128 * (o + j):128 * (o + j) + 128], ident),
                    ex, gone, sig="att_turn")
            yield "vector", [tr], []
            cp = q.dve(lambda e, o=o, n=n, bt=bt: e.tensor_copy(PTF[kt][:, 128 * o:128 * (o + n)],
                                                                PS[:, bt, 0:128 * n]), tr, gone_t, sig="att_pt")
            banks_.give(bt, cp)
            cps.append(cp)
        yield "tensor", cps, [banks_]
        bo, gone = banks_.take()
        for j in range(i + 1):
            pv = q.pe(lambda e, j=j: e.matmul(PS[:, bo, 0:128], PTF[kt][:, 128 * j:128 * j + 128],
                                              VF[s][:, 128 * j:128 * j + 128], start=(j == 0), stop=(j == i)),
                      cps, gone, sig="att_pv")
        ptf.give(kt, pv)
        t = 8 * b + i
        yield "vector", [pv], []
        x = q.dve(lambda e: e.scalar_tensor_tensor(X[:, t, :], PS[:, bo, 0:128], AM[:, k, 3:4], X[:, t, :],
                                                   ALU.mult, ALU.add), pv, ri, sig="att_x")
        banks_.give(bo, x)
        pf.give(k, x, tr)
        st[("x", t)] = x
        got = st.setdefault(("att_some", b), [])
        got.append(pv)
        if len(got) == 8:
            st[("att_done", b)] = got

    def barrier(*names):
        for e in ("tensor", "vector", "scalar", "gpsimd", "sync"):
            q.put(e, None, [(n, q.count[n]) for n in names], None, 1)
        now = max(q.clock.values())
        for e in q.clock:
            q.clock[e] = now

    ffn(False)
    barrier("x_new", "y_turn", "pv", "w2", "o_even", "o_odd")
    ab = Slots(q, range(4, 8))
    pairs = Slots(q, [(0, 1), (2, 3)])
    pf, ptf = Slots(q, range(4)), Slots(q, range(4))
    run_tasks(q, [
        ([(8 * b + i, att(b, i, ab, pairs, pf, ptf)) for b in range(NBATCH) for i in range(8)], 4),
        ([(8 * b - 8 + 4 * h, att_in(b, h, ab)) for b in range(NBATCH) for h in range(2)], 1),
    ])
    barrier("att_x", "att_pv", "att_turn", "att_proj")
    q.dve(lambda e: e.memset(QB[:], 0.0), sig="set2")
    q.dve(lambda e: e.memset(Y0[64:128, :], 0.0), sig="set2")
    barrier("set2")
    for x in (banks, t1_slots, t2_slots, sq_slots, ss_slots, p_slots, pt_slots, xn_slots, c_slots):
        x.open = {k: None for k in x.open}
    ffn(True)
    q.dma(None, ("store", q.count["store"]))

    block = ctx.enter_context(nc.Block())

    @block.sync
    def _(e):
        q.play("sync", e)

    @block.scalar
    def _(e):
        q.play("scalar", e)

    @block.vector
    def _(e):
        q.play("vector", e)

    @block.gpsimd
    def _(e):
        q.play("gpsimd", e)

    @block.tensor
    def _(e):
        q.play("tensor", e)


_INS = ['L0_attn_x', 'L0_attn_Wk', 'L0_attn_Wq', 'L0_attn_Wv', 'L0_ffn_wqkv', 'L0_ffn_q_scale', 'L0_ffn_k_scale',
        'L0_ffn_wo', 'L0_ffn_ln_g', 'L0_ffn_ln_b', 'L0_ffn_w1', 'L0_ffn_b1', 'L0_ffn_w2', 'L0_ffn_b2']


def _tables():
    f = np.float32
    half = np.arange(0, DH, 2, dtype=f)
    inv = (f(1.0) / (f(10000.0) ** (half / f(DH)))).astype(f)
    t = np.arange(SEQ, dtype=f)
    fr = t[:, None] * inv[None, :]
    fr = np.concatenate([fr, fr], -1)
    bs = ((half + f(0.4 * DH)) / f(1.4 * DH)).astype(f)
    pw = ((t - f(SEQ // 2)) / f(WIN // 2)).astype(f)
    sc = (bs[None, :] ** pw[:, None]).astype(f)
    sc = np.concatenate([sc, sc], -1)
    cos, sin = np.cos(fr).astype(f), np.sin(fr).astype(f)
    sg = np.where(np.arange(DH) < DH // 2, f(-1), f(1))[None, :]
    tabs = [f(8) * cos * sc, f(8) * sin * sc * sg, cos / sc, sin / sc * sg]
    tabs = np.stack(tabs).astype(f).reshape(4, 8, 128, DH)
    return np.ascontiguousarray(tabs.transpose(2, 0, 1, 3))


def _consts():
    c = np.zeros((128, C_END), np.float32)
    p = np.arange(128)
    c[:, C_ID:C_ID + 128] = np.eye(128)
    c[:, C_CEN:C_CEN + 128] = np.eye(128) - 1.0 / 128
    c[:, C_ONE:C_ONE + 128] = 1.0 / 128
    c[:, C_CAU:C_CAU + 128] = np.where(p[None, :] <= p[:, None], 0.0, MASKED)
    i = (p % 64)[:, None]
    ok = (p[None, :] >= i) & (p[None, :] <= i + 64)
    c[:, C_LOC:C_LOC + 128] = np.where(ok, 0.0, MASKED)
    c[:, C_LOC0:C_LOC0 + 128] = np.where(ok & (p[None, :] >= 64), 0.0, MASKED)
    return c


def kernel(**inputs):
    from contextlib import ExitStack
    import concourse.bacc as _bacc
    from concourse.bass_utils import run_bass_kernel_spmd as _run

    nc = _bacc.Bacc("TRN2", target_bir_lowering=False, num_devices=1)
    arrays, args = {}, {}
    feeds = {n: np.ascontiguousarray(inputs[n]) for n in _INS}
    feeds["table"], feeds["const"] = _tables(), _consts()
    for name, v in feeds.items():
        arrays[f"in_{name}_dram"] = v
        args[name] = nc.dram_tensor(f"in_{name}_dram", v.shape, mybir.dt.from_np(v.dtype), kind="ExternalInput").ap()
    out = nc.dram_tensor("out_0_dram", (NBATCH, SEQ, DIM), F32, kind="ExternalOutput").ap()
    with ExitStack() as ctx:
        build_program(nc, args, out, ctx)
    r = _run(nc, [arrays], core_ids=[0])
    return r.results[0]["out_0_dram"]
```

```python
import numpy as np
import concourse.bass as bass
from concourse import mybir

F32 = mybir.dt.float32
F32R = mybir.dt.float32r
BF16 = mybir.dt.bfloat16
I32 = mybir.dt.int32
ALU = mybir.AluOpType
ACT = mybir.ActivationFunctionType
AX = mybir.AxisListType

NBATCH, SEQ, DIM = 8, 1024, 128
DEPTH, HEADS, DH, WIN = 2, 8, 64, 64
INNER = HEADS * DH
HID = 341
NPAIR = HEADS // 2
HS = [128, 128, HID - 256]
CH = 256
TPC = CH // 128
WPC = CH // WIN
CPB = SEQ // CH
NCH = NBATCH * CPB
YW = SEQ + 2
NT = NBATCH * SEQ // 128
EPS = 1e-5
ASC = float(1.0 / np.sqrt(np.float32(DIM)))
MASKED = -1e30

SPAN = dict(mask_mm=216, proj=216, exp=344, pv=214, rot_add=1225, norm_mul=1001, p_scale=1001, scores=214, w1=109,
            sumsq=602, rot_cos=602, rot_sin=602, row_max=598, p_copy=598, p_copy_a=478, y_hi=200, y_lo=417,
            hn_hi=307, hn_lo=687, wa_hi=733, wa_lo=1764, w1p_hi=662, w1p_lo=1583, stage_w=4000, qk_turn=107,
            square=478, p_turn=107, wo=427, o_odd=331, w2=427, q_odd=598, q_odd_a=478, glu=396, gelu=358, o_even=264,
            v_copy=478, q_even=478, k_copy=478, ln_dve=138, att_pv=214, att_s=651, ln_rstd=464, y1=335, rstd=628,
            att_proj=500, center=427, hn=396, y0_new=396, y_last=396, row_inv=94, att_exp=800, att_pt=464,
            att_turn=107, sq_c=264, rstd_copy=264, ln_turn=107, att_qkv=478, x_new=335, y0_high=331, y_turn=107,
            y0_low=264, att_x=263, norm=83, k_head=220, v_shift=1800, store=1000, norm_max=77, rstd_all=214, ht=478,
            att_max=664, v_zero=462, var=50, b1_mm=50)
LATE = dict(tensor=dict(tensor=0, vector=196, scalar=197, gpsimd=272, sync=200),
            vector=dict(tensor=256, vector=127, scalar=128, gpsimd=203, sync=200),
            scalar=dict(tensor=230, vector=80, scalar=142, gpsimd=159, sync=200),
            gpsimd=dict(tensor=180, vector=60, scalar=75, gpsimd=60, sync=200),
            sync=dict(tensor=300, vector=300, scalar=300, gpsimd=300, sync=300))

WAIT = NBATCH
C_ID, C_CEN, C_ONE, C_KEEP, C_CAU, C_LOC, C_LOC0, C_END = 0, 128, 256, 257, 257, 385, 513, 641


class Queues:

    def __init__(self, nc, ctx):
        self.nc, self.ctx = nc, ctx
        self.items = {e: [] for e in ("tensor", "vector", "scalar", "gpsimd", "sync")}
        self.sems, self.count = {}, {}
        self.clock = {e: 0.0 for e in self.items}
        self.due = {}
        self.table = None

    def when(self, engine, *tokens):
        at = 0.0
        for t in flat(tokens):
            if t in self.due:
                end, source = self.due[t]
                at = max(at, end + LATE[source][engine])
        return at

    def put(self, engine, fn, waits, sig, inc):
        waits = flat(waits)
        self.items[engine].append((fn, waits, sig, inc))
        start = max(self.clock[engine], self.when(engine, waits))
        if sig in ("gelu", "exp", "att_exp") and (self.table == "gelu") != (sig == "gelu"):
            start += 1300
            self.table = sig
        self.clock[engine] = start + SPAN.get(sig, 100)
        if sig is None:
            return None
        if sig not in self.sems:
            self.sems[sig] = self.ctx.enter_context(self.nc.semaphore(sig))
            self.count[sig] = 0
        self.count[sig] += inc
        self.due[(sig, self.count[sig])] = (self.clock[engine], engine)
        if engine == "sync":
            self.clock[engine] = start + 600
        return (sig, self.count[sig])

    def pe(self, fn, *waits, sig=None):
        return self.put("tensor", fn, waits, sig, 1)

    def dve(self, fn, *waits, sig=None):
        return self.put("vector", fn, waits, sig, 1)

    def act(self, fn, *waits, sig=None):
        return self.put("scalar", fn, waits, sig, 1)

    def pool(self, fn, *waits, sig=None):
        return self.put("gpsimd", fn, waits, sig, 1)

    def dma(self, fn, *waits, sig=None):
        return self.put("sync", fn, waits, sig, 16)

    def play(self, engine, eng):
        waited = {}
        for fn, waits, sig, inc in self.items[engine]:
            for name, value in waits:
                if waited.get(name, 0) < value:
                    eng.wait_ge(self.sems[name], value)
                    waited[name] = value
            if fn is not None:
                ins = fn(eng)
                if sig is not None:
                    ins.then_inc(self.sems[sig], inc)


def flat(tokens):
    out = []
    for t in tokens:
        if t is None:
            continue
        if isinstance(t, tuple) and t and isinstance(t[0], str):
            out.append(t)
        else:
            out += flat(t)
    return out


class Slots:

    def __init__(self, q, places, tokens=None):
        self.q, self.open = q, {p: tokens for p in places}

    def best(self):
        return min(self.open, key=lambda p: self.q.when("tensor", self.open[p]), default=None)

    def take(self):
        p = self.best()
        return p, self.open.pop(p)

    def give(self, p, *tokens):
        self.open[p] = list(tokens)


class Pairs:

    def __init__(self, one):
        self.one = one

    @property
    def open(self):
        o = self.one.open
        return {(p, p + 1): [o[p], o[p + 1]] for p in range(0, 8, 2) if p in o and p + 1 in o}

    def best(self):
        o = self.open
        return min(o, key=lambda p: self.one.q.when("tensor", o[p]), default=None)

    def take(self):
        p = self.best()
        return p, [self.one.open.pop(p[0]), self.one.open.pop(p[1])]

    def give(self, pair, *tokens):
        for p in pair:
            self.one.give(p, *tokens)


def run_tasks(q, kinds):
    todo = [list(reversed(tasks)) for tasks, _ in kinds]
    live = []
    while True:
        for k, (_, most) in enumerate(kinds):
            while todo[k] and sum(x[0] == k for x in live) < most:
                rank, gen = todo[k].pop()
                live.append([k, rank, gen, next(gen)])
        if not live:
            return
        best = None
        for item in live:
            engine, tokens, slots = item[3]
            if callable(tokens):
                tokens = tokens()
                if tokens is None:
                    continue
                item[3] = (engine, tokens, slots)
            if any(not s.open for s in slots):
                continue
            at = max([q.clock[engine], q.when(engine, tokens)] + [q.when(engine, s.open[s.best()]) for s in slots])
            if best is None or (at, item[1]) < best[0]:
                best = ((at, item[1]), item)
        if best is None:
            raise RuntimeError("no task can go on")
        item = best[1]
        try:
            item[3] = next(item[2])
        except StopIteration:
            live.remove(item)


def build_program(nc, a, out, ctx):
    q = Queues(nc, ctx)

    def sb(name, shape, dt=F32):
        return nc.alloc_sbuf_tensor(name, [128] + shape, dt)

    X = sb("X", [NT, 128])
    Y0 = sb("Y0", [NBATCH * YW])
    QB = sb("QB", [2, NPAIR, WPC, 128])
    KT = sb("KT", [2, NPAIR, WIN + CH])
    VP = sb("VP", [2, WPC, INNER])
    OT = sb("OT", [2, NPAIR, CH])
    TAB = sb("TAB", [DEPTH, 4, 8, DH])
    WH = sb("WH", [3 * INNER], F32R)
    WL = sb("WL", [3 * INNER], F32R)
    W1H = sb("W1H", [2 * HID], F32R)
    W1L = sb("W1L", [2 * HID], F32R)
    SG = sb("SG", [3 * INNER // 2])
    YH = sb("YH", [3, 128], F32R)
    YL = sb("YL", [3, 128], F32R)
    HH = sb("HH", [CH], F32R)
    HL = sb("HL", [CH], F32R)
    WO = sb("WO", [DEPTH, NPAIR, 128])
    W2 = sb("W2", [DEPTH, 3, 128])
    WA = sb("WA", [3, 128])
    CST = sb("CST", [C_KEEP])
    IDB = sb("IDB", [128], BF16)
    MLOC = sb("MLOC", [2, NPAIR, 128], BF16)
    MCAU = sb("MCAU", [128], BF16)
    COLS = sb("COLS", [DEPTH, 16])
    NHALF = sb("NHALF", [16])
    SQ = sb("SQ", [3, INNER])
    T1 = sb("T1", [4, INNER])
    SS = sb("SS", [4, 16])
    RN = sb("RN", [4, 16])
    NW = sb("NW", [4, 2, 16])
    P = sb("P", [3, NPAIR, 128])
    PT = sb("PT", [2, NPAIR, 128])
    MX = sb("MX", [3, NPAIR])
    SM = sb("SM", [3, NPAIR])
    RI = sb("RI", [3, NPAIR])
    Y1 = sb("Y1", [2, CH + 2])
    SQL = sb("SQL", [2, CH])
    RV = sb("RV", [2, 2, 2])
    HN = sb("HN", [2, CH])
    G = sb("G", [2, 3, CH])
    ST = sb("ST", [4, 6])
    MV = sb("MV", [4, 2])
    XN = sb("XN", [4, 128])
    AM = sb("AM", [4, 4])
    PS = nc.alloc_psum_tensor("PS", [128, 8, 512], F32)

    ident = CST[:, C_ID:C_ID + 128]
    center = CST[:, C_CEN:C_CEN + 128]
    ones = CST[:, C_ONE:C_ONE + 1]

    wreg = VP[:].rearrange("p a b c -> p (a b c)")
    base = wreg[:, 0:4 * 8 * DH].rearrange("p (t m d) -> p t m d", t=4, m=8)
    msk = wreg[:, 3072:3072 + C_END - C_KEEP]
    qk = wreg[:, 2048:2048 + DEPTH * 2 * DH].rearrange("p (l s d) -> p l s d", l=DEPTH, s=2)
    xr = a["L0_attn_x"].rearrange("b (m p) d -> p (b m) d", p=128)
    half = 3 * INNER // 2
    st = {}

    def load_x(lo, hi):
        d = q.dma(lambda e: e.dma_start(X[:, lo:hi, :], xr[:, lo:hi, :]), sig=f"load_x{lo}")
        for n in range(lo, hi):
            st[("x", 0, n)] = d

    load_x(0, TPC)
    d_c = q.dma(lambda e: e.dma_start(CST[:], a["const"][:, 0:C_KEEP]), sig="load_const")
    d_wa = q.dma(lambda e: e.dma_start(SG[:], a["L0_ffn_wqkv"][0][:, 0:half]), sig="stage_w")
    load_x(TPC, 2 * TPC)
    q.dma(lambda e: e.dma_start(base, a["table"]), sig="load_scale")
    for l in range(DEPTH):
        for s, n in enumerate(("L0_ffn_q_scale", "L0_ffn_k_scale")):
            d_s = q.dma(lambda e, l=l, s=s, n=n: e.dma_start(qk[:, l, s, :], a[n][l].partition_broadcast(128)),
                        sig="load_scale")
    d_m = q.dma(lambda e: e.dma_start(msk, a["const"][:, C_KEEP:]), sig="load_mask")

    def loads():
        for lo, hi in ((2 * TPC, 8), (8, 16)):
            yield "sync", [], []
            load_x(lo, hi)
        for l in range(DEPTH):
            yield "sync", [], []
            q.dma(lambda e, l=l: e.dma_start(WO[:, l], a["L0_ffn_wo"][l].rearrange("(n p) m -> p n m", p=128)),
                  sig="load_w")
            for j in range(3):
                yield "sync", [], []
                q.dma(lambda e, l=l, j=j: e.dma_start(W2[0:HS[j], l, j, :],
                                                      a["L0_ffn_w2"][l, 128 * j:128 * j + HS[j], :]), sig="load_w")
                for s in range(2):
                    yield "sync", [], []
                    q.dma(lambda e, l=l, j=j, s=s: e.dma_start(
                        COLS[0:HS[j], l, 3 * s + j:3 * s + j + 1],
                        a["L0_ffn_b1"][l, s * HID + 128 * j:s * HID + 128 * j + HS[j]].unsqueeze(1)), sig="load_w")
            for k, n in ((6, "L0_ffn_ln_g"), (7, "L0_ffn_ln_b"), (8, "L0_ffn_b2")):
                yield "sync", [], []
                d = q.dma(lambda e, l=l, k=k, n=n: e.dma_start(COLS[:, l, k:k + 1], a[n][l].unsqueeze(1)),
                          sig="load_w")
        st[("rest",)] = d
        for k, n in enumerate(("L0_attn_Wq", "L0_attn_Wk", "L0_attn_Wv")):
            yield "sync", [], []
            st[("wa_att",)] = q.dma(lambda e, k=k, n=n: e.dma_start(WA[:, k, :], a[n]), sig="load_wa")
        for n in range(16, NT, 8):
            yield "sync", [], []
            load_x(n, n + 8)

    s_half = q.dve(lambda e: e.memset(NHALF[:], -0.5), sig="set")

    def clear(s, *waits):
        on = q.pool if s else q.dve
        return on(lambda e: e.memset(QB[:, s], 0.0), *waits, sig=f"qb_clear{s}")

    for n in range(2):
        st[("clear", n)] = clear(n)
    q.dve(lambda e: e.tensor_copy(IDB[:], ident), d_c, sig="mask")

    def tables():
        for l in range(DEPTH):
            for t in (2, 3, 0, 1):
                yield "vector", [d_s], []
                sc = qk[:, l, t // 2, :].rearrange("p (h d) -> p h d", h=2)
                if t % 2:
                    sc = sc[:, ::-1, :]
                sc = sc.unsqueeze(1).broadcast_to([128, 8, 2, 32])
                w = q.dve(lambda e, l=l, t=t, sc=sc: e.tensor_tensor(
                    TAB[:, l, t].rearrange("p m (h d) -> p m h d", h=2),
                    base[:, t].rearrange("p m (h d) -> p m h d", h=2), sc, ALU.mult), d_s, sig="table")
                st[("tab", l, t // 2)] = w
            if l == 0:
                for v, c in ((0, C_LOC), (1, C_LOC0)):
                    yield "vector", [d_m], []
                    q.dve(lambda e, v=v, c=c: e.tensor_copy(
                        MLOC[:, v], msk[:, c - C_KEEP:c - C_KEEP + 128].unsqueeze(1).broadcast_to(
                            [128, NPAIR, 128])), d_m, sig="mask")
                st[("mask",)] = q.dve(lambda e: e.tensor_copy(MCAU[:], msk[:, 0:128]), d_m, sig="mask")

    banks = Slots(q, range(8))
    t1_slots = Slots(q, range(4))
    sq_slots, yh_slots, hh_slots, sg_slots = Slots(q, range(3)), Slots(q, range(3)), Slots(q, [0]), Slots(q, [0])
    p_slots, pt_slots = Slots(q, range(3)), Slots(q, range(2))
    xn_slots = Slots(q, range(4))
    c_slots = Slots(q, range(2))
    pairs, pf, ptf = Pairs(banks), Slots(q, range(4)), Slots(q, range(4))

    def all_of(*keys):
        def get():
            out = []
            for k in keys:
                if k not in st:
                    return None
                out.append(st[k])
            return out
        return get

    def ln_rows(ph, tile):
        x = all_of(("x", ph, tile))
        yield "vector", x, [xn_slots]
        k, gone = xn_slots.take()
        w = q.dve(lambda e: e.bn_stats(ST[:, k, :], X[:, tile, :]), x(), sig="ln_dve")
        w = q.dve(lambda e: e.bn_aggr(MV[:, k, :], ST[:, k, :]), w, gone, sig="ln_dve")
        w = q.dve(lambda e: e.tensor_scalar(MV[:, k, 1:2], MV[:, k, 1:2], EPS, None, ALU.add), w, sig="ln_dve")
        yield "gpsimd", [w], []
        w = q.pool(lambda e: e.tensor_tensor(MV[:, k, 1:2], MV[:, k, 1:2], NHALF[:, 0:1], ALU.pow), w, s_half,
                   sig="ln_rstd")
        yield "vector", [w], []
        w = q.dve(lambda e: e.tensor_scalar(XN[:, k, :], X[:, tile, :], MV[:, k, 0:1], MV[:, k, 1:2],
                                            ALU.subtract, ALU.mult), w, gone, sig="ln_dve")
        return k, w

    def ln_turn(rows, bank, gone, first=0):
        for i, (k, w) in enumerate(rows, first):
            t = q.pe(lambda e, i=i, k=k: e.transpose(PS[:, bank, i * 128:i * 128 + 128], XN[:, k, :], ident),
                     w, d_c, gone, sig="ln_turn")
            xn_slots.give(k, t)
        return t

    def stage_i(ph, c):
        rows = []
        for i in range(TPC):
            rows.append((yield from ln_rows(2 * ph, c * TPC + i)))
        yield "tensor", [w for _, w in rows], [banks]
        bank, gone = banks.take()
        t = ln_turn(rows, bank, gone)
        col = (c // CPB) * YW + (c % CPB) * CH
        was = region_free(c // CPB) if ph else (lambda: [])
        yield "scalar", was, []
        yield "scalar", [t], []
        w1 = q.act(lambda e: e.copy(Y0[0:64, col:col + CH], PS[0:64, bank, 0:CH]), t, was(), sig="y0_low")
        yield "vector", [t], []
        w0 = None
        if c % CPB == 0:
            w0 = q.dve(lambda e: e.memset(Y0[64:128, col:col + 1], 0.0), was(), sig="y0_head")
        w2 = q.dve(lambda e: e.tensor_copy(Y0[64:128, col + 1:col + 1 + CH], PS[64:128, bank, 0:CH]), t, was(),
                   sig="y0_high")
        st[("y0", 2 * ph, c)] = (w0, w1, w2)
        banks.give(bank, w1, w2)

    def y0_ready(l, c):
        return all_of(*[("y0", l, n) for n in ([c] if c % CPB == 0 else [c, c - 1])])

    def counted(key, most, *tokens):
        got = st.setdefault(("some", key), [])
        got.append(tokens)
        if len(got) == most:
            st[key] = got[-6:]

    def split(hi, lo, src, waits, gone, sig):
        yield "scalar", [waits], []
        h = q.act(lambda e: e.copy(hi, src), waits, gone, sig=sig + "_hi")
        yield "gpsimd", [h], []
        low = q.pool(lambda e: e.tensor_tensor(lo, src, hi.bitcast(F32), ALU.subtract), h, waits, gone,
                     sig=sig + "_lo")
        return h, low

    def stage_wa(l, before):
        was = all_of(("proj_all", before)) if before is not None else (lambda: [])
        yield "sync", was, []
        for n in range(2):
            yield "sync", [], [sg_slots]
            _, gone = sg_slots.take()
            d = d_wa if l == 0 and n == 0 else q.dma(
                lambda e, n=n: e.dma_start(SG[:], a["L0_ffn_wqkv"][l % 2][:, half * n:half * n + half]), gone,
                sig="stage_w")
            cols = slice(half * n, half * n + half)
            h, low = yield from split(WH[:, cols], WL[:, cols], SG[:], [d], was(), "wa")
            sg_slots.give(0, h, low)
            st[("wa", l, n)] = (h, low)

    def stage_w1(l, before):
        fold = l < DEPTH
        was = all_of(("w1_all", before)) if before is not None else (lambda: [])
        yield "sync", was, [sg_slots]
        _, gone = sg_slots.take()
        d = q.dma(lambda e: e.dma_start(SG[:, 0:2 * HID], a["L0_ffn_w1"][l % 2]), gone, sig="stage_w")
        h, low = yield from split(W1H[:], W1L[:], SG[:, 0:2 * HID], [d], was(), "w1p")
        if not fold:
            sg_slots.give(0, h, low)
            st[("w1", l)] = (h, low)
            return
        rest = all_of(("rest",))
        yield "tensor", rest, [banks]
        b, gone = banks.take()
        parts = [(s, j) for s in range(2) for j in range(3)]
        for n, (s, j) in enumerate(parts):
            lo = s * HID + 128 * j
            mm = q.pe(lambda e, s=s, j=j, lo=lo, n=n: e.matmul(
                PS[0:HS[j], b, n:n + 1], SG[:, lo:lo + HS[j]], COLS[:, l, 7:8], start=True, stop=True),
                d, rest(), gone, sig="b1_mm")
        yield "vector", [mm], []
        for n, (s, j) in enumerate(parts):
            s_b1[0] = q.dve(lambda e, s=s, j=j, n=n: e.tensor_tensor(
                COLS[0:HS[j], l, 9 + n:10 + n], PS[0:HS[j], b, n:n + 1],
                COLS[0:HS[j], l, n:n + 1], ALU.add), mm, rest(), sig="b1_add")
        banks.give(b, s_b1[0])
        sg_slots.give(0, h, low, mm)
        st[("w1", l)] = (h, low, s_b1[0])

    s_b1 = [None]

    def stage_split(l, c, i):
        t = l * NCH + c
        col = (c // CPB) * YW + (c % CPB) * CH + 128 * i
        ready = y0_ready(l, c)
        yield "scalar", ready, [yh_slots]
        k, gone = yh_slots.take()
        two = yield from split(YH[:, k, :], YL[:, k, :], Y0[:, col:col + 128], ready(), gone, "y")
        counted(("y0_read", l, c), TPC, two)
        st[("y", t, i)] = two
        st[("y_slot", t, i)] = k

    def project(t, i, b, gone, x, l):
        k = st[("y_slot", t, i)]
        cols = slice(x * INNER, (x + 1) * INNER)
        for n, (y, w) in enumerate(((YH, WH), (YH, WL), (YL, WH))):
            pj = q.pe(lambda e, n=n, y=y, w=w: e.matmul(PS[:, b, :], y[:, k, :], w[:, cols], start=(n == 0),
                                                        stop=(n == 2)),
                      gone, st[("y", t, i)], st[("wa", l, 0)], st[("wa", l, 1)], sig="proj")
        got = st.setdefault(("some", "yslot", t, i), [])
        got.append(pj)
        if len(got) == 3:
            yh_slots.give(k, got)
        counted(("proj_all", l), 3 * TPC * NCH, pj)
        return pj

    def start_of(t, i, l):
        keys = [("y", t, i), ("wa", l, 0), ("wa", l, 1)]
        get = all_of(*keys)
        return lambda: None if t in AFTER and ("clear", t) not in st else get()

    def old(name, t):
        return all_of((name, t - 2)) if t >= 2 else (lambda: [])

    def stage_qk(l, c, i, x):
        t = l * NCH + c
        s = t % 2
        m = (c % CPB) * TPC + i
        col = (c // CPB) * YW + (c % CPB) * CH + 128 * i
        first = c % CPB == 0
        yield "tensor", start_of(t, i, l), [banks]
        b, gone = banks.take()
        pj = project(t, i, b, gone, x, l)
        yield "scalar", [pj], [sq_slots]
        k, gone = sq_slots.take()
        sq = q.act(lambda e: e.activation(SQ[:, k, :], PS[:, b, :], ACT.Square), pj, gone, sig="square")
        n = t * TPC + i
        r = n % 4
        was = all_of(("rn_free", n - 4)) if n >= 4 else (lambda: [])
        yield "vector", was, []
        yield "vector", [sq], []
        w = q.dve(lambda e: e.tensor_reduce(SS[:, r, 8 * x:8 * x + 8], SQ[:, k, :].rearrange("p (h d) -> p h d", h=HEADS), AX.X,
                                            ALU.add), sq, was(), sig="sumsq")
        st[("ss", n, x)] = w
        yield "vector", [sq], [t1_slots]
        k1, gone = t1_slots.take()
        tab = all_of(("tab", l % 2, x))
        yield "vector", tab, []
        tc = TAB[:, l % 2, 2 * x, m, :].unsqueeze(1).broadcast_to([128, HEADS, DH])
        ts = TAB[:, l % 2, 2 * x + 1, m, :].rearrange("p (t d) -> p t d", t=2).unsqueeze(1).broadcast_to(
            [128, HEADS, 2, 32])
        w1 = q.dve(lambda e: e.tensor_tensor(
            T1[:, k1, :].rearrange("p (h d) -> p h d", h=HEADS),
            PS[:, b, :].rearrange("p (h d) -> p h d", h=HEADS), tc, ALU.mult), sq, tab(), gone, sig="rot_cos")
        yield "vector", [sq, w], []
        k2 = k
        w2 = q.dve(lambda e: e.tensor_tensor(
            SQ[:, k2, :].rearrange("p (h t d) -> p h t d", h=HEADS, t=2),
            PS[:, b, :].rearrange("p (h t d) -> p h t d", h=HEADS, t=2)[:, :, ::-1, :], ts, ALU.mult),
            sq, w, tab(), sig="rot_sin")
        banks.give(b, w2)
        yield "gpsimd", [w1, w2], []
        ad = q.pool(lambda e: e.tensor_tensor(T1[:, k1, :], T1[:, k1, :], SQ[:, k2, :], ALU.add), w1, w2,
                    sig="rot_add")
        sq_slots.give(k2, ad)
        root = all_of(("rn", n))
        yield "gpsimd", root, []
        yield "gpsimd", [ad], []
        nm = q.pool(lambda e: e.tensor_tensor(
            T1[:, k1, :].rearrange("p (h d) -> p h d", h=HEADS), T1[:, k1, :].rearrange("p (h d) -> p h d", h=HEADS),
            RN[:, r, 8 * x:8 * x + 8].unsqueeze(2).broadcast_to([128, HEADS, DH]), ALU.mult), ad, root(),
            sig="norm_mul")
        counted(("rn_free", n), 2, nm)
        yield "tensor", [nm], [banks]
        b2, gone = banks.take()
        for p in range(NPAIR):
            tr = q.pe(lambda e, p=p: e.transpose(PS[:, b2, 128 * p:128 * p + 128],
                                                 T1[:, k1, 128 * p:128 * p + 128], ident), gone, nm, d_c,
                      sig="qk_turn")
        t1_slots.give(k1, tr)
        src = PS[:, b2, :].rearrange("p (n w i) -> p n w i", n=NPAIR, w=2)
        was = old("scored", t)
        if x == 0:
            clean = st[("clear", t)] if t < 2 or t in AFTER else None
            yield "scalar", was, []
            yield "scalar", [tr], []
            wa = q.act(lambda e: e.copy(QB[0:64, s, :, 2 * i:2 * i + 2, 0:64], src[0:64]), tr, was(), clean,
                       sig="q_even")
            wd_on = q.act if i % 2 else q.dve
            yield ("scalar" if i % 2 else "vector"), [tr], []
            wd = wd_on(lambda e: (e.copy if i % 2 else e.tensor_copy)(QB[64:128, s, :, 2 * i:2 * i + 2, 64:128], src[64:128]), tr, was(),
                       clean, sig="q_odd_a" if i % 2 else "q_odd")
            st[("q", t, i)] = (wa, wd)
            banks.give(b2, wa, wd)
            return
        if i == TPC - 1 and t >= 1 and (t - 1) % CPB != 0:
            was = all_of(("scored", t - 2), ("k_head", t - 1)) if t >= 2 else all_of(("k_head", t - 1))
        yield "scalar", was, []
        yield "scalar", [tr], []
        wk = q.act(lambda e: e.copy(KT[:, s, :, WIN + 128 * i:WIN + 128 * i + 128],
                                    PS[:, b2, :].rearrange("p (n t) -> p n t", n=NPAIR)), tr, was(),
                   sig="k_copy")
        st[("k", t, i)] = wk
        banks.give(b2, wk)

    def stage_norm(l, c, i):
        n = (l * NCH + c) * TPC + i
        r = n % 4
        ss, rn, h, u = SS[:, r, :], RN[:, r, :], NW[:, r, 0, :], NW[:, r, 1, :]
        both = all_of(("ss", n, 0), ("ss", n, 1))
        yield "vector", both, []
        w = q.dve(lambda e: e.tensor_scalar(ss, ss, 1e-24, None, ALU.max), both(), sig="norm")
        yield "vector", [w], []
        w = q.dve(lambda e: e.tensor_scalar(h.bitcast(I32), ss.bitcast(I32), 1, None, ALU.logical_shift_right), w,
                  sig="norm")
        yield "vector", [w], []
        w = q.dve(lambda e: e.tensor_scalar(rn.bitcast(I32), h.bitcast(I32), -1.0, float(0x5f3759df), ALU.mult,
                                            ALU.add), w, sig="norm")
        for _ in range(3):
            yield "vector", [w], []
            w = q.dve(lambda e: e.tensor_tensor(h, rn, rn, ALU.mult), w, sig="norm")
            yield "vector", [w], []
            w = q.dve(lambda e: e.scalar_tensor_tensor(u, h, -0.5, ss, ALU.mult, ALU.mult), w, sig="norm")
            yield "vector", [w], []
            w = q.dve(lambda e: e.scalar_tensor_tensor(rn, u, 1.5, rn, ALU.add, ALU.mult), w, sig="norm")
        st[("rn", n)] = w

    def stage_head(l, c):
        t = l * NCH + c
        s = t % 2
        was = old("scored", t)
        yield "vector", was, []
        if c % CPB == 0:
            w = q.dve(lambda e: e.memset(KT[:, s, :, 0:WIN], 0.0), was(), sig="k_head")
        else:
            before = all_of(("k", t - 1, TPC - 1))
            yield "vector", before, []
            w = q.dve(lambda e: e.tensor_copy(KT[:, s, :, 0:WIN], KT[:, 1 - s, :, CH:CH + WIN]), was(), before(),
                       sig="k_head")
        st[("k_head", t)] = w

    def stage_v(l, c, i):
        t = l * NCH + c
        s = t % 2
        col = (c // CPB) * YW + (c % CPB) * CH + 128 * i
        first = c % CPB == 0
        yield "tensor", start_of(t, i, l), [banks]
        b, gone = banks.take()
        pj = project(t, i, b, gone, 2, l)
        was = [("valued", t - 2)] if t >= 2 else []
        if i == TPC - 1 and t >= 1 and (t - 1) % CPB != 0:
            was.append(("v_shifted", t - 1, 0))
        if t < 2:
            was.append(("tab", 1, 0))
            was.append(("mask",))
        if t in AFTER:
            was.append(("att_all",))
        was = all_of(*was)
        yield "scalar", was, []
        yield "scalar", [pj], []
        wv = q.act(lambda e: e.copy(VP[:, s, 2 * i + 1, :], PS[:, b, :]), pj, was(), sig="v_copy")
        st[("v", t, i)] = wv
        banks.give(b, wv)
        sem = f"v_shift{s}{i}"
        d = q.dma(lambda e: e.dma_start(VP[64:128, s, 2 * i, :], VP[0:64, s, 2 * i + 1, :]), wv, was(),
                  sig=sem)
        z = None
        if i > 0:
            before = all_of(("v", t, i - 1))
            yield "sync", before, []
            d = q.dma(lambda e: e.dma_start(VP[0:64, s, 2 * i, :], VP[64:128, s, 2 * i - 1, :]), before(), sig=sem)
        elif first:
            yield "gpsimd", [], []
            z = q.pool(lambda e: e.memset(VP[0:64, s, 0, :], 0.0), was(), sig="v_zero")
        else:
            before = all_of(("v", t - 1, TPC - 1))
            yield "sync", before, []
            d = q.dma(lambda e: e.dma_start(VP[0:64, s, 0, :], VP[64:128, 1 - s, WPC - 1, :]), before(), sig=sem)
        st[("v_shifted", t, i)] = (d, z)

    def stage_b(l, c, w):
        t = l * NCH + c
        s = t % 2
        i = w // 2
        ready = all_of(("mask",), ("q", t, i), ("k_head", t), *[("k", t, n) for n in range(i + 1)])
        yield "tensor", ready, [banks, p_slots]
        b, gone = banks.take()
        g, gone_p = p_slots.take()
        v = 1 if (c % CPB == 0 and w == 0) else 0
        q.pe(lambda e: e.matmul(PS[:, b, :], IDB[:], MLOC[:, v].rearrange("p n k -> p (n k)"), start=True,
                                stop=True), gone, st[("mask",)], sig="mask_mm")
        for p in range(NPAIR):
            mm = q.pe(lambda e, p=p: e.matmul(PS[:, b, 128 * p:128 * p + 128], QB[:, s, p, w, :],
                                              KT[:, s, p, w * WIN:w * WIN + 128], start=False,
                                              stop=True, skip_group_check=True), ready(), sig="scores")
        done(("scored", t), mm)
        yield "vector", [mm], []
        mx = q.dve(lambda e: e.tensor_reduce(MX[:, g, :], PS[:, b, :].rearrange("p (n k) -> p n k", n=NPAIR),
                                             AX.X, ALU.max, negate=True), mm, gone_p, sig="row_max")
        yield "scalar", [mx], []
        for p in range(NPAIR):
            ex = q.act(lambda e, p=p: e.activation(P[:, g, p, :], PS[:, b, 128 * p:128 * p + 128], ACT.Exp,
                                                   bias=MX[:, g, p:p + 1], accum_out=SM[:, g, p:p + 1]),
                       mx, gone_p, sig="exp")
        banks.give(b, ex)
        yield "vector", [ex], []
        ri = q.dve(lambda e: e.reciprocal(RI[:, g, :], SM[:, g, :]), ex, sig="row_inv")
        yield "gpsimd", [ri], []
        sc = q.pool(lambda e: e.tensor_tensor(P[:, g], P[:, g], RI[:, g, :].unsqueeze(2).broadcast_to(
            [128, NPAIR, 128]), ALU.mult), ri, sig="p_scale")
        yield "tensor", [sc], [banks, pt_slots]
        b2, gone = banks.take()
        k, gone_t = pt_slots.take()
        for p in range(NPAIR):
            tr = q.pe(lambda e, p=p: e.transpose(PS[:, b2, 128 * p:128 * p + 128], P[:, g, p, :], ident),
                      gone, sc, sig="p_turn")
        p_slots.give(g, tr)
        if True:
            yield "scalar", [tr], []
            cp = q.act(lambda e: e.copy(PT[:, k].rearrange("p n k -> p (n k)"), PS[:, b2, :]), tr, gone_t,
                       sig="p_copy_a")
        else:
            yield "vector", [tr], []
            cp = q.dve(lambda e: e.tensor_copy(PT[:, k].rearrange("p n k -> p (n k)"), PS[:, b2, :]), tr, gone_t,
                       sig="p_copy")
        banks.give(b2, cp)
        vals = all_of(("v", t, i)) if w % 2 else all_of(("v_shifted", t, i))
        yield "tensor", vals, []
        yield "tensor", [cp], [banks]
        b3, gone = banks.take()
        for p in range(NPAIR):
            pv = q.pe(lambda e, p=p: e.matmul(PS[:, b3, 128 * p:128 * p + 128], VP[:, s, w, 128 * p:128 * p + 128],
                                              PT[:, k, p, :], start=True, stop=True), gone, cp, vals(), sig="pv")
        pt_slots.give(k, pv)
        done(("valued", t), pv)
        src = PS[:, b3, :].rearrange("p (n k) -> p n k", n=NPAIR)
        was = old("wo", t)
        yield "scalar", was, []
        yield "scalar", [pv], []
        o1 = q.act(lambda e: e.copy(OT[0:64, s, :, WIN * w:WIN * w + WIN], src[0:64, :, 0:64]), pv, was(),
                   sig="o_even")
        yield "vector", [pv], []
        o2 = q.dve(lambda e: e.tensor_copy(OT[64:128, s, :, WIN * w:WIN * w + WIN], src[64:128, :, 64:128]), pv,
                   was(), sig="o_odd")
        banks.give(b3, o1, o2)
        done(("windows", t), (o1, o2))

    def done(key, token):
        got = st.setdefault(("some", key), [])
        got.append(token)
        if len(got) == WPC:
            st[key] = got

    def stage_c(l, c):
        t = l * NCH + c
        s = t % 2
        col = (c // CPB) * YW + (c % CPB) * CH
        last, final, wl = l % 2 == 1, l == 2 * DEPTH - 1, l % 2
        ready = all_of(("windows", t), ("rest",))
        yield "tensor", ready, [banks, c_slots]
        z, gone_c = c_slots.take()
        b, gone = banks.take()
        for p in range(NPAIR):
            mm = q.pe(lambda e, p=p: e.matmul(PS[:, b, 0:CH], WO[:, wl, p, :], OT[:, s, p, :], start=(p == 0),
                                              stop=(p == NPAIR - 1)), gone, ready(), sig="wo")
        st[("wo", t)] = mm
        y0 = st[("y0", l, c)]
        was = []
        if c % CPB:
            was.append(("y1", t - 1))
        if t >= 2:
            was.append(("y1_free", t - 2))
        if t >= 1 and (t - 1) % CPB:
            was.append(("y1", t - 1))
        was = all_of(*was)
        yield "vector", was, []
        yield "vector", [mm], []
        if c % CPB == 0:
            h = q.dve(lambda e: e.memset(Y1[64:128, s, 0:1], 0.0), was(), sig="y1_head")
        else:
            h = q.dve(lambda e: e.tensor_copy(Y1[64:128, s, 0:1], Y1[64:128, 1 - s, CH:CH + 1]), was(),
                      sig="y1_head")
        q.dve(lambda e: e.tensor_tensor(Y1[0:64, s, 0:CH], PS[0:64, b, 0:CH], Y0[0:64, col:col + CH], ALU.add),
              mm, y0, was(), sig="y1")
        y1 = q.dve(lambda e: e.tensor_tensor(Y1[64:128, s, 1:CH + 1], PS[64:128, b, 0:CH],
                                             Y0[64:128, col + 1:col + 1 + CH], ALU.add), mm, y0, was(), sig="y1")
        st[("y1", t)] = (h, y1)
        banks.give(b, y1)
        yield "tensor", [y1, h], [banks]
        bc, gone = banks.take()
        ce = q.pe(lambda e: e.matmul(PS[:, bc, 0:CH], center, Y1[:, s, 0:CH], start=True, stop=True), gone, y1, h,
                  sig="center")
        yield "scalar", [ce], []
        sq = q.act(lambda e: e.activation(SQL[:, z], PS[:, bc, 0:CH], ACT.Square), ce, gone_c, sig="sq_c")
        yield "tensor", [sq], [banks]
        bv, gone = banks.take()
        for i in range(TPC):
            v = q.pe(lambda e, i=i: e.matmul(PS[:, bv, i:i + 1], SQL[:, z, 128 * i:128 * i + 128], ones,
                                             start=True, stop=True), sq, gone, sig="var")
        yield "vector", [v], []
        w = q.dve(lambda e: e.tensor_scalar(RV[:, z, 0, :], PS[:, bv, 0:TPC], EPS, None, ALU.add), v, gone_c,
                  sig="var_eps")
        banks.give(bv, w)
        yield "gpsimd", [w], []
        w = q.pool(lambda e: e.tensor_tensor(RV[:, z, 1, :], RV[:, z, 0, :], NHALF[:, 0:TPC], ALU.pow), w,
                   sig="rstd")
        yield "tensor", [w], [banks]
        br, gone = banks.take()
        for i in range(TPC):
            al = q.pe(lambda e, i=i: e.matmul(PS[:, br, 128 * i:128 * i + 128],
                                              RV[:, z, 1, i:i + 1].broadcast_to([128, 128]), ident, start=True,
                                              stop=True), w, gone, sig="rstd_all")
        yield "scalar", [al], []
        w = q.act(lambda e: e.copy(SQL[:, z], PS[:, br, 0:CH]), al, v, sig="rstd_copy")
        banks.give(br, w)
        yield "vector", [w], []
        hn = q.dve(lambda e: e.scalar_tensor_tensor(HN[:, z], PS[:, bc, 0:CH], COLS[:, wl, 6:7], SQL[:, z], ALU.mult,
                                                    ALU.mult), w, gone_c, sig="hn")
        banks.give(bc, hn)
        yield "scalar", all_of(("w1", l)), [hh_slots]
        _, gone_h = hh_slots.take()
        two = yield from split(HH[:], HL[:], HN[:, z], [hn], gone_h, "hn")
        w1_ready = st[("w1", l)]

        def up(bank, off, part, j, gone):
            lo = part * HID + 128 * j
            for n, (w, h) in enumerate(((W1H, HH), (W1L, HH), (W1H, HL))):
                mm = q.pe(lambda e, n=n, w=w, h=h: e.matmul(PS[0:HS[j], bank, off:off + CH], w[:, lo:lo + HS[j]],
                                                            h[:], start=(n == 0), stop=(n == 2)),
                          two, w1_ready, gone, sig="w1")
            return mm

        yield "tensor", [two], [banks]
        b6, gone = banks.take()
        up(b6, 0, 1, 0, gone)
        g1 = up(b6, CH, 1, 1, gone)
        yield "tensor", [two], [banks]
        b7, gone = banks.take()
        up(b7, 0, 1, 2, gone)
        g2 = up(b7, CH, 0, 2, gone)
        yield "scalar", [g2], []
        for j, (bank, off, w) in enumerate(((b6, 0, g1), (b6, CH, g1), (b7, 0, g2))):
            ge = q.act(lambda e, j=j, bank=bank, off=off: e.activation(
                G[0:HS[j], z, j, :], PS[0:HS[j], bank, off:off + CH], ACT.Gelu, bias=COLS[0:HS[j], wl, 12 + j:13 + j]),
                w, w1_ready, gone_c, sig="gelu")
        yield "tensor", [ge], []
        up(b6, 0, 0, 0, ge)
        a1 = up(b6, CH, 0, 1, ge)
        hh_slots.give(0, a1)
        counted(("w1_all", l), NCH, a1)
        yield "vector", [a1], []
        for j, (bank, off, w) in enumerate(((b6, 0, a1), (b6, CH, a1), (b7, CH, g2))):
            hw = q.dve(lambda e, j=j, bank=bank, off=off: e.scalar_tensor_tensor(
                G[0:HS[j], z, j, :], PS[0:HS[j], bank, off:off + CH], COLS[0:HS[j], wl, 9 + j:10 + j], G[0:HS[j], z, j, :],
                ALU.add, ALU.mult), w, ge, gone_c, sig="glu")
        banks.give(b6, hw)
        banks.give(b7, hw)
        yield "tensor", [hw], [banks]
        bw, gone = banks.take()
        for j in range(3):
            mm = q.pe(lambda e, j=j: e.matmul(PS[:, bw, 0:CH], W2[0:HS[j], wl, j, :], G[0:HS[j], z, j, :],
                                              start=(j == 0), stop=(j == 2)), hw, gone, sig="w2")
        b2 = COLS[:, wl, 8:9]
        if not last:
            reads = [("y0_read", l, c)] + ([("y0_read", l, c + 1)] if (c + 1) % CPB else [])
            reads = all_of(*reads)
            yield "vector", reads, []
            yield "vector", [mm], []
            q.dve(lambda e: e.scalar_tensor_tensor(Y0[0:64, col:col + CH], PS[0:64, bw, 0:CH], b2[0:64],
                                                   Y1[0:64, s, 0:CH], ALU.add, ALU.add), mm, reads(), y1,
                  sig="y0_new")
            y = q.dve(lambda e: e.scalar_tensor_tensor(Y0[64:128, col + 1:col + 1 + CH], PS[64:128, bw, 0:CH],
                                                       b2[64:128], Y1[64:128, s, 1:CH + 1], ALU.add, ALU.add),
                      mm, y1, sig="y0_new")
            st[("y0", l + 1, c)] = y
            st[("y1_free", t)] = y
            banks.give(bw, y)
            c_slots.give(z, y, mm)
            return
        yield "vector", [mm], []
        q.dve(lambda e: e.scalar_tensor_tensor(HN[0:64, z], PS[0:64, bw, 0:CH], b2[0:64], Y1[0:64, s, 0:CH],
                                               ALU.add, ALU.add), mm, y1, gone_c, sig="y_last")
        y = q.dve(lambda e: e.scalar_tensor_tensor(HN[64:128, z], PS[64:128, bw, 0:CH], b2[64:128],
                                                   Y1[64:128, s, 1:CH + 1], ALU.add, ALU.add), mm, y1, gone_c,
                  sig="y_last")
        st[("y1_free", t)] = y
        banks.give(bw, y)
        yield "tensor", [y], [banks]
        bt, gone = banks.take()
        for i in range(TPC):
            tr = q.pe(lambda e, i=i: e.transpose(PS[:, bt, 128 * i:128 * i + 128], HN[:, z, 128 * i:128 * i + 128],
                                                 ident), y, gone, sig="y_turn")
        yield "vector", [tr], []
        xs = X[:, c * TPC:(c + 1) * TPC, :]
        x = q.dve(lambda e: e.scalar_tensor_tensor(xs, PS[:, bt, 0:CH].rearrange("p (t d) -> p t d", t=TPC), 0.5, xs,
                                                   ALU.mult, ALU.add), tr, sig="x_new")
        banks.give(bt, x)
        c_slots.give(z, x, mm)
        for i in range(TPC):
            st[("x", l, c * TPC + i)] = x
        if final:
            q.dma(lambda e: e.dma_start(outr[:, TPC * c:TPC * (c + 1), :], X[:, TPC * c:TPC * (c + 1), :]), x,
                  sig="store")

    outr = out.rearrange("b (m p) d -> p (b m) d", p=128)

    AFTER = (2 * NCH, 2 * NCH + 1)
    bigq = QB[:].rearrange("p a b c d -> p (a b c d)")
    bigv = VP[:].rearrange("p a b c -> p (a b c)")
    rows_of = [Y0[:, k * YW:k * YW + SEQ] for k in range(NBATCH)]
    HT, QT, KF, VF = [[rows_of[0], rows_of[1]], [rows_of[2], rows_of[5]], [rows_of[3], rows_of[6]],
                      [rows_of[4], rows_of[7]]]
    PF = [bigq[:, k * SEQ:(k + 1) * SEQ] for k in range(4)]
    PTF = [bigv[:, k * SEQ:(k + 1) * SEQ] for k in range(4)]

    def region_free(k):
        return all_of(("ht_free", NBATCH - 2 + k)) if k < 2 else all_of(("att_done", NBATCH - 2 + k // 5))

    def regions_read(s):
        t = DEPTH * NCH - NCH
        ks = [0, 2, 3, 4] if s == 0 else [1, 5, 6, 7]
        return [(n, *at) for k in ks for c in range(CPB * k, CPB * k + CPB)
                for n, *at in (("y0_read", DEPTH - 1, c), ("y1", t + c))]

    def att_in(b, h):
        s = b % 2
        was = all_of(*regions_read(s)) if b < 2 else all_of(("att_done", b - 2))
        bk = None
        for n in range(2):
            rows = []
            for i in range(2):
                rows.append((yield from ln_rows(1, 8 * b + 4 * h + 2 * n + i)))
            yield "tensor", [w for _, w in rows], ([banks] if n == 0 else [])
            if n == 0:
                bk, gone = banks.take()
            t = ln_turn(rows, bk, gone, 2 * n)
        yield "scalar", was, []
        yield "scalar", [t], []
        ht = q.act(lambda e: e.copy(HT[s][:, 512 * h:512 * h + 512], PS[:, bk, :]), t, was(), sig="ht")
        banks.give(bk, ht)
        got = []
        d_w = st[("wa_att",)]
        for x, dst in ((0, QT), (1, KF), (2, VF)):
            yield "tensor", [ht], [banks]
            bx, gone = banks.take()
            if x < 2:
                p = q.pe(lambda e, bx=bx, x=x: e.matmul(PS[:, bx, :], WA[:, x, :], HT[s][:, 512 * h:512 * h + 512],
                                                        start=True, stop=True), ht, gone, d_w, sig="att_proj")
            else:
                for i in range(4):
                    p = q.pe(lambda e, bx=bx, i=i: e.matmul(
                        PS[:, bx, 128 * i:128 * i + 128], HT[s][:, 512 * h + 128 * i:512 * h + 128 * i + 128],
                        WA[:, 2, :], start=True, stop=True), ht, gone, d_w, sig="att_proj")
            yield "scalar", [p], []
            w = q.act(lambda e, bx=bx, dst=dst: e.copy(dst[s][:, 512 * h:512 * h + 512], PS[:, bx, :]), p, was(),
                      sig="att_qkv")
            banks.give(bx, w)
            got.append(w)
        st[("att_in", b, h)] = got
        counted(("ht_free", b), 2, p)

    def att(b, i):
        s = b % 2
        nk = 128 * (i + 1)
        t = DEPTH * NCH
        free = [(n, t - k) for n in ("scored", "valued") for k in (1, 2)]
        ready = all_of(*[("att_in", b, h) for h in range(i // 4 + 1)], *free)
        places = pairs if i >= 4 else banks
        yield "tensor", ready, [places, pf]
        taken, gone = places.take()
        ba, bb = taken if i >= 4 else (taken, None)
        k, gone_p = pf.take()
        for o in range(0, nk, 512):
            bank = ba if o == 0 else bb
            n = min(512, nk - o)
            diag = o + n == nk
            if diag:
                q.pe(lambda e, n=n, bank=bank: e.matmul(PS[:, bank, n - 128:n], IDB[:], MCAU[:], start=True,
                                                        stop=True), st[("mask",)], gone)
            mm = q.pe(lambda e, o=o, n=n, bank=bank, diag=diag: e.matmul(
                PS[:, bank, 0:n], QT[s][:, 128 * i:128 * i + 128], KF[s][:, o:o + n], start=not diag,
                stop=True, skip_group_check=True), ready(), gone, sig="att_s")
        src = PS[:, ba:ba + 2, :].rearrange("p b k -> p (b k)")[:, 0:nk] if i >= 4 else PS[:, ba, 0:nk]
        yield "vector", [mm], []
        mx = q.dve(lambda e: e.tensor_reduce(AM[:, k, 0:1], src, AX.X, ALU.max, negate=True), mm, gone_p,
                   sig="att_max")
        mx = q.dve(lambda e: e.tensor_scalar(AM[:, k, 1:2], AM[:, k, 0:1], ASC, None, ALU.mult), mx, sig="att_bias")
        yield "scalar", [mx], []
        ex = q.act(lambda e: e.activation(PF[k][:, 0:nk], src, ACT.Exp, bias=AM[:, k, 1:2], scale=ASC,
                                          accum_out=AM[:, k, 2:3]), mx, gone_p, ready(), sig="att_exp")
        places.give(taken, ex)
        yield "vector", [ex], []
        ri = q.dve(lambda e: e.reciprocal(AM[:, k, 3:4], AM[:, k, 2:3]), ex, sig="att_inv")
        cps = []
        for o in range(0, i + 1, 4):
            n = min(4, i + 1 - o)
            yield "tensor", [ex], [banks] + ([ptf] if o == 0 else [])
            bt, gone = banks.take()
            if o == 0:
                kt, gone_t = ptf.take()
            for j in range(n):
                tr = q.pe(lambda e, o=o, j=j, bt=bt: e.transpose(
                    PS[:, bt, 128 * j:128 * j + 128], PF[k][:, 128 * (o + j):128 * (o + j) + 128], ident),
                    ex, gone, sig="att_turn")
            yield "vector", [tr], []
            cp = q.dve(lambda e, o=o, n=n, bt=bt: e.tensor_copy(PTF[kt][:, 128 * o:128 * (o + n)],
                                                                PS[:, bt, 0:128 * n]), tr, gone_t, ready(), sig="att_pt")
            banks.give(bt, cp)
            cps.append(cp)
        yield "tensor", cps, [banks]
        bo, gone = banks.take()
        for j in range(i + 1):
            pv = q.pe(lambda e, j=j: e.matmul(PS[:, bo, 0:128], PTF[kt][:, 128 * j:128 * j + 128],
                                              VF[s][:, 128 * j:128 * j + 128], start=(j == 0), stop=(j == i)),
                      cps, gone, sig="att_pv")
        ptf.give(kt, pv)
        t = 8 * b + i
        yield "vector", [pv], []
        x = q.dve(lambda e: e.scalar_tensor_tensor(X[:, t, :], PS[:, bo, 0:128], AM[:, k, 3:4], X[:, t, :],
                                                   ALU.mult, ALU.add), pv, ri, sig="att_x")
        banks.give(bo, x)
        pf.give(k, x, tr)
        st[("x", 2, t)] = x
        counted(("att_done", b), 8, pv)
        counted(("att_all",), NT, [pv, tr])

    def clear_again():
        for s in range(2):
            over = all_of(("att_all",))
            yield ("gpsimd" if s else "vector"), over, []
            st[("clear", 2 * NCH + s)] = clear(s, over())

    phases = [0] * DEPTH + [WAIT] * DEPTH
    steps = [(l, c, l * NCH + c + phases[l]) for l in range(2 * DEPTH) for c in range(NCH)]
    run_tasks(q, [
        ([(r + 3.25, stage_c(l, c)) for l, c, r in steps], 2),
        ([(r + 1 + w / WPC, stage_b(l, c, w)) for l, c, r in steps for w in range(WPC)], 3),
        ([(r, stage_head(l, c)) for l, c, r in steps], 1),
        ([(r + i / TPC + -0.5, stage_norm(l, c, i)) for l, c, r in steps for i in range(TPC)], 3),
        ([(r + i / TPC + 0, stage_qk(l, c, i, x)) for l, c, r in steps for i in range(TPC) for x in (1, 0)], 6),
        ([(r + i / TPC + -1.5, stage_split(l, c, i)) for l, c, r in steps for i in range(TPC)], 3),
        ([(NCH * l, w) for l in range(2 * DEPTH)
          for w in (stage_wa(l, l - 1 if l else None), stage_w1(l, l - 1 if l else None))], 1),
        ([(r + i / TPC + 0.25, stage_v(l, c, i)) for l, c, r in steps for i in range(TPC)], 2),
        ([(ph * (2 * NCH + WAIT) + c + -1.5, stage_i(ph, c)) for ph in range(2) for c in range(NCH)], 3),
        ([(0, tables())], 1),
        ([(0, loads())], 1),
        ([(2 * NCH + b + i / 8, att(b, i)) for b in range(NBATCH) for i in range(8)], 4),
        ([(2 * NCH + b + h / 2 - 1, att_in(b, h)) for b in range(NBATCH) for h in range(2)], 1),
        ([(2 * NCH + WAIT, clear_again())], 1),
    ])
    q.dma(None, ("store", q.count["store"]))

    block = ctx.enter_context(nc.Block())

    @block.sync
    def _(e):
        q.play("sync", e)

    @block.scalar
    def _(e):
        q.play("scalar", e)

    @block.vector
    def _(e):
        q.play("vector", e)

    @block.gpsimd
    def _(e):
        q.play("gpsimd", e)

    @block.tensor
    def _(e):
        q.play("tensor", e)


_INS = ['L0_attn_x', 'L0_attn_Wk', 'L0_attn_Wq', 'L0_attn_Wv', 'L0_ffn_wqkv', 'L0_ffn_q_scale', 'L0_ffn_k_scale',
        'L0_ffn_wo', 'L0_ffn_ln_g', 'L0_ffn_ln_b', 'L0_ffn_w1', 'L0_ffn_b1', 'L0_ffn_w2', 'L0_ffn_b2']


def _tables():
    f = np.float32
    half = np.arange(0, DH, 2, dtype=f)
    inv = (f(1.0) / (f(10000.0) ** (half / f(DH)))).astype(f)
    t = np.arange(SEQ, dtype=f)
    fr = t[:, None] * inv[None, :]
    fr = np.concatenate([fr, fr], -1)
    bs = ((half + f(0.4 * DH)) / f(1.4 * DH)).astype(f)
    pw = ((t - f(SEQ // 2)) / f(WIN // 2)).astype(f)
    sc = (bs[None, :] ** pw[:, None]).astype(f)
    sc = np.concatenate([sc, sc], -1)
    cos, sin = np.cos(fr).astype(f), np.sin(fr).astype(f)
    sg = np.where(np.arange(DH) < DH // 2, f(-1), f(1))[None, :]
    tabs = [f(8) * cos * sc, f(8) * sin * sc * sg, cos / sc, sin / sc * sg]
    tabs = np.stack(tabs).astype(f).reshape(4, 8, 128, DH)
    return np.ascontiguousarray(tabs.transpose(2, 0, 1, 3))


def _consts():
    c = np.zeros((128, C_END), np.float32)
    p = np.arange(128)
    c[:, C_ID:C_ID + 128] = np.eye(128)
    c[:, C_CEN:C_CEN + 128] = np.eye(128) - 1.0 / 128
    c[:, C_ONE] = 1.0 / 128
    c[:, C_CAU:C_CAU + 128] = np.where(p[None, :] <= p[:, None], 0.0, MASKED)
    i = (p % 64)[:, None]
    ok = (p[None, :] >= i) & (p[None, :] <= i + 64)
    c[:, C_LOC:C_LOC + 128] = np.where(ok, 0.0, MASKED)
    c[:, C_LOC0:C_LOC0 + 128] = np.where(ok & (p[None, :] >= 64), 0.0, MASKED)
    return c


def kernel(**inputs):
    from contextlib import ExitStack
    import concourse.bacc as _bacc
    from concourse.bass_utils import run_bass_kernel_spmd as _run

    nc = _bacc.Bacc("TRN2", target_bir_lowering=False, num_devices=1)
    arrays, args = {}, {}
    feeds = {n: np.ascontiguousarray(inputs[n]) for n in _INS}
    feeds["table"], feeds["const"] = _tables(), _consts()
    for name, v in feeds.items():
        arrays[f"in_{name}_dram"] = v
        args[name] = nc.dram_tensor(f"in_{name}_dram", v.shape, mybir.dt.from_np(v.dtype), kind="ExternalInput").ap()
    out = nc.dram_tensor("out_0_dram", (NBATCH, SEQ, DIM), F32, kind="ExternalOutput").ap()
    with ExitStack() as ctx:
        build_program(nc, args, out, ctx)
    r = _run(nc, [arrays], core_ids=[0])
    return r.results[0]["out_0_dram"]
```
